# Optimizing a Trainium2 kernel written in Bass

```python
import numpy as np
import jax
import jax.numpy as jnp

def _softmax(x, axis=-1):
    return jax.nn.softmax(x, axis=axis)

def _gelu(x):
    return jax.nn.gelu(x, approximate=True)

def _silu(x):
    return jax.nn.silu(x)

def _sigmoid(x):
    return jax.nn.sigmoid(x)

def _layernorm(x, axis=-1, eps=1e-05):
    m = jnp.mean(x, axis=axis, keepdims=True)
    v = jnp.var(x, axis=axis, keepdims=True)
    return (x - m) / jnp.sqrt(v + eps)

def _scatter_add(tgt, idx, src, axis=0):
    return tgt.at[idx].add(src)

def _segment_sum(src, seg, n):
    return jax.ops.segment_sum(src, seg, n)
kernel_name = 'mk_seq_preln_d1_jaxref_r8_cdaf72'

def setup_inputs(seed: int=0):
    np.random.seed(seed)
    _w = jnp.asarray

    def _L0_attn_setup():
        import jax, jax.numpy as jnp
        import numpy as np
        E = 128
        H = 16
        HD = E // H
        MAX_REL = 20
        key = jax.random.key(seed)
        ks = jax.random.split(key, 12)
        B, S = (4, 128)

        def lin_w(k):
            return jax.random.normal(k, (E, E), dtype=jnp.float32) * (1.0 / np.sqrt(E))
        return {'hidden_states': jax.random.normal(ks[0], (B, S, E), dtype=jnp.float32), 'Wq': lin_w(ks[1]), 'bq': jnp.zeros((E,), jnp.float32), 'Wk': lin_w(ks[2]), 'bk': jnp.zeros((E,), jnp.float32), 'Wv': lin_w(ks[3]), 'bv': jnp.zeros((E,), jnp.float32), 'Wo': lin_w(ks[4]), 'bo': jnp.zeros((E,), jnp.float32), 'rel_k': jax.random.uniform(ks[5], (2 * MAX_REL + 1, HD), jnp.float32, -0.24, 0.24), 'rel_v': jax.random.uniform(ks[6], (2 * MAX_REL + 1, HD), jnp.float32, -0.24, 0.24)}
    _L0_attn_in = _L0_attn_setup()

    def _L0_ffn_setup():
        import jax, jax.numpy as jnp
        import numpy as np
        DIM = 128
        HIDDEN = 384
        SCALE = 1.0 / 127.0

        def _dequant(w_int, dtype):
            return w_int.astype(dtype) * jnp.asarray(SCALE, dtype)
        key = jax.random.key(seed)
        k_x, k_g, k_u, k_d = jax.random.split(key, 4)
        x = jax.random.normal(k_x, (4, 256, DIM), dtype=jnp.float32)
        w_gate = jax.random.randint(k_g, (HIDDEN, DIM), -127, 128, dtype=jnp.int32)
        w_up = jax.random.randint(k_u, (HIDDEN, DIM), -127, 128, dtype=jnp.int32)
        w_down = jax.random.randint(k_d, (DIM, HIDDEN), -127, 128, dtype=jnp.int32)
        return {'x': x, 'w_gate': w_gate, 'w_up': w_up, 'w_down': w_down}
    _L0_ffn_in = _L0_ffn_setup()
    _d = {'L0_attn_hidden_states': _L0_attn_in['hidden_states'], 'L0_attn_Wq': _L0_attn_in['Wq'], 'L0_attn_bq': _L0_attn_in['bq'], 'L0_attn_Wk': _L0_attn_in['Wk'], 'L0_attn_bk': _L0_attn_in['bk'], 'L0_attn_Wv': _L0_attn_in['Wv'], 'L0_attn_bv': _L0_attn_in['bv'], 'L0_attn_Wo': _L0_attn_in['Wo'], 'L0_attn_bo': _L0_attn_in['bo'], 'L0_attn_rel_k': _L0_attn_in['rel_k'], 'L0_attn_rel_v': _L0_attn_in['rel_v'], 'L0_ffn_w_gate': _L0_ffn_in['w_gate'], 'L0_ffn_w_up': _L0_ffn_in['w_up'], 'L0_ffn_w_down': _L0_ffn_in['w_down']}
    _x0 = _d['L0_attn_hidden_states']
    _d['L0_attn_hidden_states'] = jax.random.normal(jax.random.fold_in(jax.random.key(seed), 1), (16, 512, 128), dtype=_x0.dtype)
    del _x0
    return _d

def reference(L0_attn_hidden_states, L0_attn_Wq, L0_attn_bq, L0_attn_Wk, L0_attn_bk, L0_attn_Wv, L0_attn_bv, L0_attn_Wo, L0_attn_bo, L0_attn_rel_k, L0_attn_rel_v, L0_ffn_w_gate, L0_ffn_w_up, L0_ffn_w_down):

    def _L0_attn_ref(hidden_states, Wq, bq, Wk, bk, Wv, bv, Wo, bo, rel_k, rel_v):
        import jax, jax.numpy as jnp
        import numpy as np
        E = 128
        H = 16
        HD = E // H
        MAX_REL = 20
        B, S, _ = hidden_states.shape
        scale = jnp.sqrt(jnp.float32(HD))

        def proj(W, b):
            return (hidden_states @ W.T + b).reshape(B, S, H, HD).transpose(0, 2, 1, 3)
        q = proj(Wq, bq)
        k = proj(Wk, bk)
        v = proj(Wv, bv)
        pos = jnp.arange(S)
        idx = jnp.clip(pos[None, :] - pos[:, None], -MAX_REL, MAX_REL) + MAX_REL
        rk2 = rel_k[idx]
        rv2 = rel_v[idx]
        attn1 = jnp.einsum('bhqd,bhkd->bhqk', q, k)
        attn2 = jnp.einsum('bhqd,qkd->bhqk', q, rk2)
        attn = jax.nn.softmax((attn1 + attn2) / scale, axis=-1)
        w1 = jnp.einsum('bhqk,bhkd->bhqd', attn, v)
        w2 = jnp.einsum('bhqk,qkd->bhqd', attn, rv2)
        x = (w1 + w2).transpose(0, 2, 1, 3).reshape(B, S, E)
        out = x @ Wo.T + bo
        return out

    def _L0_ffn_ref(x, w_gate, w_up, w_down):
        import jax, jax.numpy as jnp
        import numpy as np
        DIM = 128
        HIDDEN = 384
        SCALE = 1.0 / 127.0

        def _dequant(w_int, dtype):
            return w_int.astype(dtype) * jnp.asarray(SCALE, dtype)
        wg = _dequant(w_gate, x.dtype)
        wu = _dequant(w_up, x.dtype)
        wd = _dequant(w_down, x.dtype)
        gate = jnp.einsum('bsd,hd->bsh', x, wg)
        up = jnp.einsum('bsd,hd->bsh', x, wu)
        h = jax.nn.silu(gate) * up
        return jnp.einsum('bsh,dh->bsd', h, wd)
    x = L0_attn_hidden_states
    x = x + _L0_attn_ref(_layernorm(x, axis=-1), L0_attn_Wq, L0_attn_bq, L0_attn_Wk, L0_attn_bk, L0_attn_Wv, L0_attn_bv, L0_attn_Wo, L0_attn_bo, L0_attn_rel_k, L0_attn_rel_v)
    x = x + _L0_ffn_ref(_layernorm(x, axis=-1), L0_ffn_w_gate, L0_ffn_w_up, L0_ffn_w_down)
    return x

_drawn_inputs = setup_inputs


def setup_inputs(seed=0):
    import zlib

    import numpy as np

    out = dict(_drawn_inputs(seed))
    spreads = {'L0_attn_bq': (0.0, 0.53),
     'L0_attn_bk': (0.0, 0.8),
     'L0_attn_bv': (0.0, 0.1),
     'L0_attn_bo': (0.0, 0.1)}
    factors = {'L0_attn_rel_k': 2.784}
    for name, (base, spread) in spreads.items():
        noise = np.random.default_rng([zlib.crc32(name.encode()), seed]).standard_normal(out[name].shape)
        drawn = base * np.exp(spread * noise) if base else spread * noise
        out[name] = jnp.asarray(drawn.astype(out[name].dtype))
    for name, factor in factors.items():
        out[name] = (out[name] * factor).astype(out[name].dtype)
    return out
```

```python
from contextlib import ExitStack

import numpy as np

import concourse.bass as bass
from concourse import mybir

F32 = mybir.dt.float32
BF16 = mybir.dt.bfloat16
I32 = mybir.dt.int32
ALU = mybir.AluOpType
ACT = mybir.ActivationFunctionType
AX_X = mybir.AxisListType.X

P = 128
B, S, E = 16, 512, 128
H, HD = 16, 8
REL = 20
NREL = 2 * REL + 1
T = S // P
U = B * T
F = 384
FC = F // P
EPS = 1e-5

SLOTS = 6
K_SLOT = {0: (0, 3, 5), 1: (1, 4), 2: (2,)}
Q_SLOT = {0: (0, 1, 2), 1: (3, 4), 2: (5,)}
OPR = SLOTS * HD
GROW = 96
DROW = GROW + 3
ROWS = DROW + 3

HG = 8
NG = H // HG
SUB = T * NG
QB = 16
WB = 4
V16 = 16
NQ4 = 4

ZLO_W, ZLO_0 = 272, 144
ZHI_W, ZHI_0 = 144, -16
EXT_0 = 176
EXT = 2 * EXT_0 + 1
VW = 2 * T * H * V16
VGW = VW + 4 * T * H


def bc(ap, axis, n):
    ap = ap.unsqueeze(axis)
    shape = list(ap.shape)
    shape[axis] = n
    return ap.to_broadcast(shape)


def batches(eng, batch):
    batch(0)
    with eng.Fori(1, B) as b:
        batch(b)


def wait_past(eng, sem, count):
    if not (isinstance(count, int) and count == 0):
        eng.wait_ge(sem, count)


class Memory:

    def __init__(self, nc, ctx):
        self.nc, self.ctx = nc, ctx

    def sb(self, name, shape, dt=F32):
        return self.ctx.enter_context(self.nc.sbuf_tensor(name, shape, dt))

    def ps(self, name, shape, dt=F32):
        return self.ctx.enter_context(self.nc.psum_tensor(name, shape, dt))

    def sem(self, name):
        return self.ctx.enter_context(self.nc.semaphore(name))


def setup_constants(nc, m, k, d):
    s_ld, s_id, s_z, s_v = m.sem("su_loaded"), m.sem("su_pool"), m.sem("su_zero"), m.sem("su_vector")
    ones = m.sb("su_ones", [P, P])
    wgi = m.sb("su_wgi", [P, F], I32)
    wui = m.sb("su_wui", [P, F], I32)
    wdi = m.sb("su_wdi", [P, FC, P], I32)
    bkc = m.sb("su_bk", [P, 1])
    rkc, rkj = m.sb("su_rkc", [P, NREL]), m.sb("su_rkj", [P, 2])
    bvb, rvb = m.sb("su_bvb", [P, P]), m.sb("su_rvb", [P, 2, HD])
    rkd = m.sb("su_rkd", [P, NREL])
    hm = m.sb("su_hm", [P, H])
    loads = []

    def toeplitz_k(dst, width, first):
        for jr in range(QB):
            src = d["rkx"][:, EXT_0 + first + jr:EXT_0 + first + jr + width]
            loads.append((dst[jr * HD:(jr + 1) * HD, :], src))

    def toeplitz_v(dst, nq, first):
        src = bass.AP(d["rvx"].tensor, (EXT_0 + first) * HD, [[HD, P], [1, nq * HD]])
        loads.append((dst, src))

    toeplitz_k(k["zlo"][:, :], ZLO_W, 1 - QB - ZLO_0)
    toeplitz_k(k["zhi"][:, :], ZHI_W, 1 - QB - ZHI_0)
    toeplitz_v(k["tvd"][:, :], P, 1 - P)
    toeplitz_v(k["tvm"][:, :], REL, 1 - P - P + P - REL)
    toeplitz_v(k["tvp"][:, :], REL, 1)
    for n in ("wq", "wk", "wv", "wo"):
        loads.append((k[n][:, :], d[n]))
    loads += [(wgi[:, :], d["wg"]), (wui[:, :], d["wu"]), (wdi[:, :, :], d["wd"].rearrange("(c p) e -> p c e", p=P)),
              (k["bq"][:, :], d["bq"]), (bkc[:, :], d["bk"]), (rkc[:, :], d["rkh"]), (rkj[:, :], d["rkj"]),
              (bvb[:, :], d["bv"].to_broadcast([P, P])), (k["bo"][:, :], d["bo"].to_broadcast([P, P])),
              (rvb[:, 0, :], d["rv"][0:1, :].to_broadcast([P, HD])),
              (rvb[:, 1, :], d["rv"][NREL - 1:NREL, :].to_broadcast([P, HD]))]
    with nc.Block() as block:
        @block.sync
        def _(sp):
            for dst, src in loads:
                sp.dma_start(dst, src).then_inc(s_ld, 16)

        @block.gpsimd
        def _(pool):
            n = 0

            def link(ins):
                nonlocal n
                n += 1
                ins.then_inc(s_id, 1)
                pool.wait_ge(s_id, n)

            link(nc.gpsimd.memset(ones[:, :], 1.0))
            link(nc.gpsimd.memset(k["ident"][:, :], 0.0))
            link(nc.gpsimd.affine_select(out=k["ident"][:, :], in_=k["ident"][:, :], compare_op=ALU.not_equal, fill=1.0,
                                         base=0, pattern=[[-1, P]], channel_multiplier=1))
            link(nc.gpsimd.affine_select(out=k["qmask"][:, :], in_=ones[:, 0:QB], compare_op=ALU.is_ge, fill=0.0,
                                         base=-HD * (QB - 1), pattern=[[HD, QB]], channel_multiplier=1))
            link(nc.gpsimd.affine_select(out=k["qmask"][:, :], in_=k["qmask"][:, :], compare_op=ALU.is_ge, fill=0.0,
                                         base=HD * QB - 1, pattern=[[-HD, QB]], channel_multiplier=-1))
            for b in range(NQ4):
                w = k["wmask"][32 * b:32 * b + 32, :]
                link(nc.gpsimd.affine_select(out=w, in_=ones[32 * b:32 * b + 32, 0:WB], compare_op=ALU.is_ge, fill=0.0,
                                             base=-HD * (WB - 1), pattern=[[HD, WB]], channel_multiplier=1))
                link(nc.gpsimd.affine_select(out=w, in_=w, compare_op=ALU.is_ge, fill=0.0,
                                             base=HD * WB - 1, pattern=[[-HD, WB]], channel_multiplier=-1))
            link(nc.gpsimd.memset(k["red"][:, :, :], 0.0))

        @block.vector
        def _(dve):
            n = 0

            def link(ins):
                nonlocal n
                n += 1
                ins.then_inc(s_v, 1)
                dve.wait_ge(s_v, n)

            dve.wait_ge(s_ld, 16 * len(loads))
            dve.wait_ge(s_id, 5 + 2 * NQ4 + 1)
            link(nc.vector.tensor_scalar(k["zlo"][:, :], k["zlo"][:, :], rkj[:, 0:1], None, ALU.subtract))
            link(nc.vector.tensor_scalar(k["zhi"][:, :], k["zhi"][:, :], rkj[:, 1:2], None, ALU.subtract))
            for name, nq, side in (("tvd", P, 0), ("tvm", REL, 0), ("tvp", REL, 1)):
                v = k[name][:, :].rearrange("p (q d) -> p q d", d=HD)
                link(nc.vector.tensor_tensor(v, v, bc(rvb[:, side, :], 1, nq), ALU.subtract))
            link(nc.vector.tensor_tensor(k["bk0"][:, :], bkc[:, :], rkc[:, 0:1], ALU.add))
            for side in range(2):
                link(nc.vector.tensor_tensor(k["bv2"][:, side, :].rearrange("p (h d) -> p h d", d=HD),
                                             bvb[:, :].rearrange("p (h d) -> p h d", d=HD),
                                             bc(rvb[:, side, :], 1, H), ALU.add))
            link(nc.vector.tensor_reduce(hm[:, :], k["ident"][:, :].rearrange("p (d h) -> p h d", h=H), AX_X, ALU.add))
            link(nc.vector.tensor_scalar(rkd[:, :], rkc[:, :], rkc[:, 0:1], None, ALU.subtract))
            link(nc.vector.tensor_scalar(k["relend"][:, :], hm[:, :], rkd[:, NREL - 1:NREL], None, ALU.mult))
            for i in range(2):
                link(nc.vector.tensor_tensor(k["relbd"][:, i, :].rearrange("p (h r) -> p h r", h=H),
                                             bc(rkd[:, 1 + REL * i:1 + REL * (i + 1)], 1, H),
                                             bc(hm[:, :], 2, REL), ALU.mult))
            link(nc.vector.tensor_reduce(k["red"][:, :, 0:HD],
                                         k["ident"][:, :].rearrange("p (b j d) -> p b d j", b=NQ4, d=HD), AX_X, ALU.add))
            for dst, src in ((k["wg"][:, :], wgi[:, :]), (k["wu"][:, :], wui[:, :]), (k["wd"][:, :, :], wdi[:, :, :])):
                link(nc.vector.tensor_copy(dst, src))
                link(nc.vector.tensor_scalar(dst, dst, float(np.float32(1.0 / 127.0)), None, ALU.mult))
            link(nc.vector.memset(k["eps"][:, :], EPS))


def layernorm_vector(nc, dve, x, xn, tmp, chain, s_var, s_std, n, first_use=None):
    for t in range(T):
        ins = nc.vector.bn_stats(tmp["st"][:, t, :], x[:, t, :])
    chain(ins)
    nc.vector.memset(tmp["gap"][:, :], 0.0)
    for t in range(T):
        ins = nc.vector.bn_aggr(tmp["mv"][:, t, :], tmp["st"][:, t, :])
    ins.then_inc(s_var, 1)
    dve.wait_ge(s_std, n + 1)
    chain(nc.vector.reciprocal(tmp["rstd"][:, :], tmp["std"][:, :]))
    if first_use is not None:
        first_use()
    for t in range(T):
        ins = nc.vector.tensor_scalar(xn[:, t, :], x[:, t, :], tmp["mv"][:, t, 0:1], tmp["rstd"][:, t:t + 1],
                                      ALU.subtract, ALU.mult)
    return ins


def stage_project(nc, m, k, d):
    x, xn = m.sb("a_x", [P, T, E]), m.sb("a_xn", [P, T, E])
    xnT = m.sb("a_xnT", [P, S])
    qf = m.sb("a_qf", [P, 2, S])
    db = m.sb("a_db", [P, 3, T * H], BF16)
    dr = m.sb("a_dr", [P, T * H])
    res = m.sb("a_res", [P, S])
    parts = m.sb("a_parts", [P, 2, 3, S], BF16)
    vt = m.sb("a_vt", [P, VGW])
    gr = m.sb("a_gr", [P, 2, T, H])
    tmp = {"st": m.sb("a_st", [P, T, 6]), "mv": m.sb("a_mv", [P, T, 2]), "std": m.sb("a_std", [P, T]),
           "rstd": m.sb("a_rstd", [P, T]), "gap": m.sb("a_gap", [P, 1])}
    pT, pq, pk, pv = (m.ps(f"a_p{n}", [P, S]) for n in "tqkv")
    pd = m.ps("a_pd", [P, T * H])
    pr = [m.ps(f"a_pr{n}", [P, S]) for n in range(2)]
    names = ("x_in", "var", "std", "xn", "xT", "xTs", "proj", "fevac", "split", "vdone", "ends", "rel", "relmax", "out", "dv")
    s = {n: m.sem("a_s_" + n) for n in names}
    NCH = 2 + 3 * 2 + 4 + 1
    NOUT = 3 + 4 + 1 + 1

    with nc.Block() as block:
        @block.sync
        def _(sp):
            def batch(b):
                wait_past(sp, s["xn"], b)
                sp.dma_start(x[:, :, :], d["x"][bass.ds(b, 1)].rearrange("o (t p) e -> p (o t) e", p=P)).then_inc(s["x_in"], 16)
                sp.wait_ge(s["split"], 2 * b + 2)
                for o, name in enumerate(("qop", "kop")):
                    for part, slots in (Q_SLOT if o == 0 else K_SLOT).items():
                        dst = d[name][bass.ds(b, 1)].rearrange("o s p t -> p (o s) t")
                        src = parts[:, o, part, :]
                        step = slots[1] - slots[0] if len(slots) > 1 else 1
                        even = slots[:2] if o and part == 0 else slots
                        sp.dma_start(dst[:, even[0]:even[-1] + 1:step, :],
                                     bc(src, 1, len(even))).then_inc(s["out"], 16)
                        for n in slots[len(even):]:
                            sp.dma_start(dst[:, n, :], src).then_inc(s["out"], 16)
                sp.dma_start(d["qf"][bass.ds(b, 1)].rearrange("o p t -> p (o t)"), qf[:, 0, :]).then_inc(s["out"], 16)
                sp.wait_ge(s["vdone"], b + 1)
                sp.dma_start(d["vg"][bass.ds(b, 1)].rearrange("o p t -> p (o t)"), vt[:, :]).then_inc(s["out"], 16)

            batches(sp, batch)
            sp.wait_ge(s["out"], 16 * NOUT * B)

        @block.tensor
        def _(pe):
            def batch(b):
                pe.wait_ge(s["xn"], b + 1)
                wait_past(pe, s["xTs"], b)
                for t in range(T):
                    ins = nc.tensor.transpose(pT[:, t * P:(t + 1) * P], xn[:, t, :], k["ident"][:, :])
                ins.then_inc(s["xT"], 1)
                pe.wait_ge(s["xTs"], b + 1)
                wait_past(pe, s["fevac"], b)
                wait_past(pe, s["vdone"], b)
                nc.tensor.matmul(pq[:, :], k["wq"][:, :], xnT[:, :], start=True, stop=True)
                nc.tensor.matmul(pk[:, :], k["wk"][:, :], xnT[:, :], start=True, stop=True)
                for t in range(T):
                    ins = nc.tensor.matmul(pv[:, t * P:(t + 1) * P], xnT[:, t * P:(t + 1) * P], k["wv"][:, :],
                                           start=True, stop=True)
                ins.then_inc(s["proj"], 1)
                pe.wait_ge(s["fevac"], b + 1)
                for t in range(T):
                    ins = nc.tensor.matmul(pd[:, t * H:(t + 1) * H], qf[:, 0, t * P:(t + 1) * P], k["relend"][:, :],
                                           start=True, stop=True)
                ins.then_inc(s["ends"], 1)
                pe.wait_ge(s["split"], 2 * b + 1)
                for t in range(T):
                    wait_past(pe, s["relmax"], T * b + t)
                    for i in range(2):
                        ins = nc.tensor.matmul(pr[i][:, 0:H * REL], parts[:, 0, 0, t * P:(t + 1) * P],
                                               k["relbd"][:, i, :], start=True, stop=True)
                    ins.then_inc(s["rel"], 1)

            batches(pe, batch)

        @block.scalar
        def _(act):
            def batch(b):
                act.wait_ge(s["var"], b + 1)
                nc.scalar.activation(tmp["std"][:, :], tmp["mv"][:, :, 1], ACT.Sqrt, bias=k["eps"][:, 0:1]).then_inc(s["std"], 1)
                act.wait_ge(s["xT"], b + 1)
                nc.scalar.copy(xnT[:, :], pT[:, :]).then_inc(s["xTs"], 1)
                act.wait_ge(s["proj"], b + 1)
                wait_past(act, s["out"], 16 * NOUT * b)
                wait_past(act, s["split"], 2 * b)
                wait_past(act, s["ends"], b)
                nc.scalar.activation(qf[:, 0, :], pq[:, :], ACT.Identity, bias=k["bq"][:, 0:1])
                nc.scalar.activation(qf[:, 1, :], pk[:, :], ACT.Identity, bias=k["bk0"][:, 0:1]).then_inc(s["fevac"], 1)

            batches(act, batch)

        @block.vector
        def _(dve):
            nc.vector.memset(vt[:, 0:VW], 0.0).then_inc(s["dv"], 1)
            dve.wait_ge(s["dv"], 1)
            nc.vector.memset(vt[:, 0:VW].rearrange("p (n c) -> p n c", c=V16)[:, :, HD:HD + 1], 1.0).then_inc(s["dv"], 1)
            dve.wait_ge(s["dv"], 2)
            def batch(b):
                n = 0

                def chain(ins):
                    nonlocal n
                    n += 1
                    ins.then_inc(s["dv"], 1)
                    dve.wait_ge(s["dv"], b * NCH + 2 + n)

                dve.wait_ge(s["x_in"], 16 * b + 16)
                wait_past(dve, s["xT"], b)
                layernorm_vector(nc, dve, x, xn, tmp, chain, s["var"], s["std"], b).then_inc(s["xn"], 1)
                dve.wait_ge(s["fevac"], b + 1)
                for o in range(2):
                    chain(nc.vector.tensor_copy(parts[:, o, 0, :], qf[:, o, :]))
                    chain(nc.vector.tensor_tensor(res[:, :], qf[:, o, :], parts[:, o, 0, :], ALU.subtract))
                    chain(nc.vector.tensor_copy(parts[:, o, 1, :], res[:, :]))
                    nc.vector.tensor_tensor(parts[:, o, 2, :], res[:, :], parts[:, o, 1, :], ALU.subtract).then_inc(s["split"], 1)
                for side in range(2):
                    out = vt[:, side * VW // 2:(side + 1) * VW // 2].rearrange("p (t h c) -> p t h c", t=T, h=H)
                    for t in range(T):
                        nc.vector.tensor_tensor(out[:, t, :, 0:HD], pv[:, t * P:(t + 1) * P].rearrange("p (h d) -> p h d", h=H),
                                                k["bv2"][:, side, :].rearrange("p (h d) -> p h d", h=H), ALU.add)
                dve.wait_ge(s["ends"], b + 1)
                chain(nc.vector.tensor_copy(db[:, 0, :], pd[:, :]))
                chain(nc.vector.tensor_tensor(dr[:, :], pd[:, :], db[:, 0, :], ALU.subtract))
                chain(nc.vector.tensor_copy(db[:, 1, :], dr[:, :]))
                chain(nc.vector.tensor_tensor(db[:, 2, :], dr[:, :], db[:, 1, :], ALU.subtract))
                nc.vector.tensor_copy(vt[:, VW + T * H:VGW], db[:, :, :].rearrange("p c n -> p (c n)"))
                for t in range(T):
                    dve.wait_ge(s["rel"], T * b + t + 1)
                    for i in range(2):
                        ins = nc.vector.reduce_max(gr[:, i, t, :], pr[i][:, 0:H * REL].rearrange("p (h r) -> p h r", h=H), AX_X)
                    ins.then_inc(s["relmax"], 1)
                dve.wait_ge(s["relmax"], T * b + T)
                chain(nc.vector.tensor_tensor(gr[:, 0, :, :], gr[:, 0, :, :], gr[:, 1, :, :], ALU.max))
                nc.vector.tensor_scalar(vt[:, VW:VW + T * H].rearrange("p (t h) -> p t h", t=T), gr[:, 0, :, :], 0.0, None,
                                        ALU.max).then_inc(s["vdone"], 1)

            batches(dve, batch)


def stage_attend(nc, m, k, d):
    K = [m.sb(f"b_k{p}", [P, H, S], BF16) for p in range(2)]
    Q = [m.sb(f"b_q{p}", [P, H, S], BF16) for p in range(2)]
    VG = [m.sb(f"b_v{p}", [P, VGW]) for p in range(2)]
    QD = [m.sb(f"b_qd{p}", [P, H, P]) for p in range(2)]
    PR = [m.sb(f"b_p{p}", [P, T, H, P]) for p in range(2)]
    WM = m.sb("b_wm", [P, P // QB, H, WB])
    XT = m.sb("b_xt", [P, NQ4 * P])
    XN = [m.sb(f"b_xn{p}", [P, E]) for p in range(2)]
    RD = m.sb("b_rd", [P, H])
    MX = [m.sb(f"b_mx{p}", [P, H]) for p in range(2)]
    nm, r1, r2 = (m.sb(f"b_{n}", [P, H]) for n in ("nm", "r1", "r2"))
    NP = m.sb("b_np", [P, 6, H], BF16)
    MT = m.sb("b_mt", [6 * H, P], BF16)
    idb = m.sb("b_idb", [P, P], BF16)
    SC = [m.ps(f"b_s{p}", [P, 2, S]) for p in range(2)]
    PA = [m.ps(f"b_a{p}", [P, S]) for p in range(2)]
    PV = m.ps("b_pv", [P, NQ4 * P])
    MI = m.ps("b_mi", [P, S])
    names = ("init", "a_ready", "a_used", "s_ready", "p_ready", "w_ready", "w_masked", "pv_ready", "xt_ready", "rd",
             "mp_ready", "mt_ready", "mt_copied", "xtt_ready", "norm", "m_out", "m_in", "xo_out0", "xo_out1",
             "qd_masked", "dv", "kq_in0", "kq_in1", "v_in0", "v_in1", "qd_in0", "qd_in1")
    s = {n: m.sem("b_s_" + n) for n in names}
    kq_in, v_in, qd_in, xo_out = ([s[f"{n}{p}"] for p in range(2)] for n in ("kq_in", "v_in", "qd_in", "xo_out"))
    NKQ, NQD = 2, QB
    MCH = 6
    SCALE = float(1.0 / np.sqrt(np.float32(HD)))

    def par(v, n):
        return (v // n) % 2, v // (2 * n)

    class At:

        def __init__(self, it, c):
            self.it, self.c = it, c

        def plus(self, n):
            return At(self.it, self.c + n)

        def count(self, per=1, extra=0):
            return self.it * (PER * per) + (self.c * per + extra)

        def even(self, n):
            return self.it * (PER // (2 * n)) + self.c // (2 * n)

    PER = 2 * T

    def run(eng, unit):
        for c in range(PER):
            unit(At(0, c), True, False)
        with eng.Fori(1, U // PER - 1) as it:
            for c in range(PER):
                unit(At(it, c), False, False)
        for c in range(PER):
            unit(At(U // PER - 1, c), False, True)

    def exists(at, first, last, shift):
        n = at.c + shift
        return not (first and n < 0) and not (last and n >= PER)

    def since_start(first, at, n):
        return not first or at.c >= n

    def window(t, i):
        return abs(t - i) <= 1

    with nc.Block() as block:
        @block.sync
        def _(sp):
            def load_kq(at):
                p = (at.c // T) % 2
                dram = at.it * 2 + at.c // T
                for name, dst in (("kop", K[p]), ("qop", Q[p])):
                    sp.dma_start(dst[0:OPR, :, :], d[name][bass.ds(dram, 1)].rearrange("o s (d h) t -> (o s d) h t", h=H))\
                        .then_inc(kq_in[p], 16)

            def load_v(at):
                p = (at.c // T) % 2
                sp.dma_start(VG[p][:, :], d["vg"][bass.ds(at.it * 2 + at.c // T, 1)].rearrange("o p c -> (o p) c")).then_inc(v_in[p], 16)

            def load_qd(at):
                p = at.c % 2
                i = at.c % T
                src = d["qf"][bass.ds(at.it * 2 + at.c // T, 1), :, i * P:(i + 1) * P].rearrange("o (d h) t -> (o d) h t", h=H)
                for jr in range(QB):
                    sp.dma_start(QD[p][jr * HD:(jr + 1) * HD, :, :], src).then_inc(qd_in[p], 16)

            def guard_rows(at):
                sp.wait_ge(s["mt_copied"], at.count(1, 1))
                sp.dma_start(d["gt"][at.c % 2], MT[:, :]).then_inc(s["m_out"], 16)
                sp.wait_ge(s["m_out"], at.count(16, 16))
                p, i = (at.c // T) % 2, at.c % T
                sp.dma_start(Q[p][GROW:ROWS, :, i * P:(i + 1) * P], d["gt"][at.c % 2].rearrange("(c h) q -> c h q", h=H))\
                    .then_inc(s["m_in"], 16)

            sp.wait_ge(s["init"], 4)
            load_kq(At(0, 0))
            load_v(At(0, 0))
            load_qd(At(0, 0))
            load_kq(At(0, T))
            load_v(At(0, T))
            guard_rows(At(0, 0))

            def unit(at, first, last):
                if since_start(first, at, 1):
                    sp.wait_ge(s["s_ready"], at.count(SUB))
                if exists(at, first, last, 1):
                    load_qd(at.plus(1))
                if at.c % T == 0 and since_start(first, at, T) and exists(at, first, last, T):
                    load_kq(at.plus(T))
                    sp.wait_ge(s["w_ready"], at.count(1))
                    load_v(at.plus(T))
                if since_start(first, at, 2):
                    sp.wait_ge(s["norm"], at.count(1, -1))
                    sp.dma_start(d["xo"][bass.ds(at.count(1, -2), 1)].rearrange("o p c -> (o p) c"), XN[at.c % 2][:, :])\
                        .then_inc(xo_out[at.c % 2], 16)
                if exists(at, first, last, 1):
                    guard_rows(at.plus(1))

            run(sp, unit)
            for u in (U - 2, U - 1):
                sp.wait_ge(s["norm"], u + 1)
                sp.dma_start(d["xo"][u], XN[u % 2][:, :]).then_inc(xo_out[u % 2], 16)
            for p in range(2):
                sp.wait_ge(xo_out[p], 16 * U // 2)

        @block.gpsimd
        def _(pool):
            for p in range(2):
                ins = nc.gpsimd.memset(Q[p][:, :, :], 0.0)
            ins.then_inc(s["init"], 1)

            def unit(at, first, last):
                p = at.c % 2
                pool.wait_ge(qd_in[p], at.even(1) * (16 * NQD) + 16 * NQD)
                v = QD[p][:, :, :].rearrange("p h (b j) -> p (h b) j", j=QB)
                nc.gpsimd.tensor_tensor(v, v, bc(k["qmask"][:, :], 1, H * P // QB), ALU.mult).then_inc(s["qd_masked"], 1)

            run(pool, unit)

        @block.tensor
        def _(pe):
            def row_scores(at, heads):
                p, i = (at.c // T) % 2, at.c % T
                if at.c % T == 0 and heads[0] == 0:
                    pe.wait_ge(kq_in[p], (at.even(T) + 1) * (16 * NKQ))
                for h in heads:
                    if not (isinstance(at.it, int) and at.it * PER + at.c == 0 and h < 2):
                        pe.wait_ge(s["a_used"], at.count(H, h - 1))
                    nc.tensor.matmul(PA[h % 2][:, :], Q[p][0:GROW, h, i * P:(i + 1) * P], K[p][0:GROW, h, :],
                                     start=True, stop=True).then_inc(s["a_ready"], 1)

            def scores(at, c, first):
                t, g, i, p = c // NG, c % NG, at.c % T, (at.c // T) % 2
                out = SC[c % 2]
                if since_start(first, at, 1) or c >= 2:
                    pe.wait_ge(s["p_ready"], at.count(SUB, c - 1))
                if c == 0:
                    pe.wait_ge(s["m_in"], at.count(16, 16))
                rows = DROW if t <= i else ROWS
                for hh in range(HG):
                    h = HG * g + hh
                    lhs = K[p][0:rows, h, t * P:(t + 1) * P]
                    if window(t, i):
                        for half in range(2):
                            q0 = i * P + half * 64
                            ins = nc.tensor.matmul(out[:, half, hh * 64:(hh + 1) * 64], lhs, Q[p][0:rows, h, q0:q0 + 64],
                                                   start=hh == 0, stop=True, skip_group_check=True)
                    else:
                        ins = nc.tensor.matmul(out[:, hh // 4, (hh % 4) * P:(hh % 4 + 1) * P], lhs,
                                               Q[p][0:rows, h, i * P:(i + 1) * P],
                                               start=hh % 4 == 0, stop=True, skip_group_check=True)
                if window(t, i):
                    if c == NG * max(i - 1, 0):
                        pe.wait_ge(s["qd_masked"], at.count(1, 1))
                    blocks = {0: range(P // QB), -1: range(2), 1: range(P // QB - 2, P // QB)}[t - i]
                    for b in blocks:
                        z, z0 = (k["zlo"], ZLO_0) if t <= i else (k["zhi"], ZHI_0)
                        x0 = z0 + (t - i) * P - QB * b
                        o = out[:, b // 4, :].rearrange("p (h q) -> p h q", h=HG)[:, :, (b % 4) * QB:(b % 4 + 1) * QB]
                        ins = nc.tensor.matmul(o, z[:, x0:x0 + P], QD[at.c % 2][:, HG * g:HG * g + HG, b * QB:(b + 1) * QB],
                                               start=False, stop=True, skip_group_check=True)
                ins.then_inc(s["s_ready"], 1)

            def value_products(at, t, first):
                i, p = at.c % T, (at.c // T) % 2
                v = VG[p][:, 0:VW].rearrange("p (s t h c) -> p s t h c", s=2, t=T, h=H)
                if t == 0 and since_start(first, at, 1):
                    pe.wait_ge(s["xt_ready"], at.count(1))
                if t == 0 and i == 0:
                    pe.wait_ge(v_in[p], (at.even(T) + 1) * 16)
                pe.wait_ge(s["p_ready"], at.count(SUB, NG * (t + 1)))
                for g in range(H // NQ4):
                    for a in range(NQ4):
                        h = NQ4 * a + g
                        nc.tensor.matmul(PV[32 * a:32 * a + V16, g * P:(g + 1) * P], v[:, 0 if t <= i else 1, t, h, :],
                                         PR[at.c % 2][:, t, h, :], start=(t == 0 and g == 0), stop=True,
                                         skip_group_check=True)

            def relative_values(at, first):
                i = at.c % T
                for qb in range(P // WB):
                    jobs = [(i, k["tvd"], P - WB - WB * qb)]
                    if i > 0 and qb < REL // WB:
                        jobs.append((i - 1, k["tvm"], REL - WB - WB * qb))
                    if i < T - 1 and qb >= (P - REL) // WB:
                        jobs.append((i + 1, k["tvp"], P - WB - WB * qb))
                    a, grp = qb % NQ4, qb // NQ4
                    for n, (t, tab, q0) in enumerate(jobs):
                        ins = nc.tensor.matmul(MI[32 * a:32 * a + 32, grp * H * WB:(grp + 1) * H * WB],
                                               tab[:, q0 * HD:(q0 + WB) * HD], PR[at.c % 2][:, t, :, qb * WB:(qb + 1) * WB],
                                               start=n == 0, stop=n == len(jobs) - 1)
                ins.then_inc(s["w_ready"], 1)

            def relative_value_sums(at):
                pe.wait_ge(s["w_masked"], at.count(1, 1))
                for b in range(NQ4):
                    for a in range(NQ4):
                        o = PV[32 * a:32 * a + V16, :].rearrange("p (h g b q) -> p h g b q", h=NQ4, b=NQ4, q=WB)[:, :, :, b, :]
                        ins = nc.tensor.matmul(o, k["red"][:, b, :], WM[:, :, NQ4 * a:NQ4 * a + NQ4, :].rearrange("p g h q -> p h g q"),
                                               start=False, stop=True, skip_group_check=True)
                ins.then_inc(s["pv_ready"], 1)

            def guard_transpose(at):
                pe.wait_ge(s["mp_ready"], at.count(1, 1))
                nc.tensor.transpose(MIB, NP[:, :, :].rearrange("p c h -> p (c h)"), idb[:, :]).then_inc(s["mt_ready"], 1)

            def output_transposes(at):
                pe.wait_ge(s["xt_ready"], at.count(1, 1))
                for g in range(NQ4):
                    ins = nc.tensor.transpose(MI[:, g * P:(g + 1) * P], XT[:, g * P:(g + 1) * P], k["ident"][:, :])
                ins.then_inc(s["xtt_ready"], 1)

            MIB = MI[0:6 * H, 0:P // 2].bitcast(BF16)
            pe.wait_ge(s["init"], 4)
            row_scores(At(0, 0), range(H))
            guard_transpose(At(0, 0))
            row_scores(At(0, 1), range(H))

            def unit(at, first, last):
                before = at.plus(-1)
                for c in range(SUB):
                    if exists(at, first, last, 2):
                        row_scores(at.plus(2), range(2 * c, 2 * c + 2))
                    scores(at, c, first)
                    if exists(at, first, last, -1):
                        if c == 0:
                            value_products(before, T - 1, first)
                        if c == 1:
                            if since_start(first, at, 2):
                                pe.wait_ge(s["norm"], at.count(1, -1))
                            elif first:
                                pe.wait_ge(s["mt_copied"], 1)
                            relative_values(before, first)
                        if c == 2:
                            relative_value_sums(before)
                    if c == 3:
                        if exists(at, first, last, 1):
                            if not (first and at.c == 0):
                                pe.wait_ge(s["w_masked"], at.count(1))
                            else:
                                pe.wait_ge(s["mt_copied"], 1)
                            guard_transpose(at.plus(1))
                        value_products(at, 0, first)
                    if c == 4 and exists(at, first, last, -1):
                        if exists(at, first, last, 1):
                            pe.wait_ge(s["mt_copied"], at.count(1, 2))
                        output_transposes(before)
                    if c == 5:
                        value_products(at, 1, first)
                    if c == 7:
                        value_products(at, 2, first)

            run(pe, unit)
            end = At(U // PER - 1, PER - 1)
            value_products(end, T - 1, False)
            pe.wait_ge(s["norm"], U - 1)
            relative_values(end, False)
            relative_value_sums(end)
            output_transposes(end)

        @block.scalar
        def _(act):
            def exponentials(at, c, first):
                t, g, i = c // NG, c % NG, at.c % T
                act.wait_ge(s["s_ready"], at.count(SUB, c + 1))
                if c == 0 and since_start(first, at, 2):
                    act.wait_ge(s["w_ready"], at.count(1, -1))
                out = PR[at.c % 2][:, t, HG * g:HG * g + HG, :]
                if window(t, i):
                    src = SC[c % 2][:, :, :].rearrange("p c (h q) -> p c h q", h=HG)
                    out = out.rearrange("p h (c q) -> p c h q", c=2)
                else:
                    src = SC[c % 2][:, :, :].rearrange("p c (h q) -> p (c h) q", q=P)
                nc.scalar.activation(out, src, ACT.Exp, scale=SCALE).then_inc(s["p_ready"], 1)

            def guard_copy(at):
                act.wait_ge(s["mt_ready"], at.count(1, 1))
                if not (isinstance(at.it, int) and at.it == 0 and at.c == 0):
                    act.wait_ge(s["m_out"], at.count(16))
                nc.scalar.copy(MT[:, :], MI[0:6 * H, 0:P // 2].bitcast(BF16)).then_inc(s["mt_copied"], 1)

            def output_copy(at, first):
                act.wait_ge(s["pv_ready"], at.count(1, 1))
                if since_start(first, at, 1):
                    act.wait_ge(s["xtt_ready"], at.count(1))
                nc.scalar.copy(XT[:, :], PV[:, :]).then_inc(s["xt_ready"], 1)

            guard_copy(At(0, 0))

            def unit(at, first, last):
                for c in range(SUB):
                    exponentials(at, c, first)
                    if c == 2 and exists(at, first, last, -1):
                        output_copy(at.plus(-1), first)
                    if c == 3 and exists(at, first, last, 1):
                        guard_copy(at.plus(1))

            run(act, unit)
            output_copy(At(U // PER - 1, PER - 1), False)

        @block.vector
        def _(dve):
            for p in range(2):
                nc.vector.memset(K[p][0:GROW, :, :], 0.0)
            for p in range(2):
                nc.vector.memset(K[p][GROW:P, :, :], 1.0).then_inc(s["init"], 1)
            nc.vector.memset(PV[:, :], 0.0)
            nc.vector.tensor_copy(idb[:, :], k["ident"][:, :]).then_inc(s["init"], 1)

            def row_max(at, heads):
                for h in heads:
                    dve.wait_ge(s["a_ready"], at.count(H, h + 1))
                    nc.vector.reduce_max(MX[at.c % 2][:, h:h + 1], PA[h % 2][:, :], AX_X).then_inc(s["a_used"], 1)

            def link(at, n, ins):
                ins.then_inc(s["dv"], 1)
                dve.wait_ge(s["dv"], at.count(MCH - 1, n))

            def guard_parts(at):
                p, i = (at.c // T) % 2, at.c % T
                dve.wait_ge(s["a_used"], at.count(H, H))
                if i == 0:
                    dve.wait_ge(v_in[p], (at.even(T) + 1) * 16)
                if not (isinstance(at.it, int) and at.it == 0 and at.c == 0):
                    dve.wait_ge(s["mt_ready"], at.count(1))
                g = VG[p][:, VW + i * H:VW + (i + 1) * H]
                nc.vector.tensor_copy(NP[:, 3:6, :], VG[p][:, VW + T * H:VGW].rearrange("p (c t h) -> p c t h", c=3, t=T)[:, :, i, :])
                link(at, 1, nc.vector.scalar_tensor_tensor(out=nm[:, :], in0=MX[at.c % 2][:, :], scalar=-1.0, in1=g,
                                                           op0=ALU.mult, op1=ALU.subtract))
                link(at, 2, nc.vector.tensor_copy(NP[:, 0, :], nm[:, :]))
                link(at, 3, nc.vector.tensor_tensor(r1[:, :], nm[:, :], NP[:, 0, :], ALU.subtract))
                link(at, 4, nc.vector.tensor_copy(NP[:, 1, :], r1[:, :]))
                link(at, 5, nc.vector.tensor_tensor(r2[:, :], r1[:, :], NP[:, 1, :], ALU.subtract))
                nc.vector.tensor_copy(NP[:, 2, :], r2[:, :]).then_inc(s["mp_ready"], 1)

            def keep_values(at, first):
                dve.wait_ge(s["w_ready"], at.count(1, 1))
                if since_start(first, at, 1):
                    dve.wait_ge(s["pv_ready"], at.count(1))
                nc.vector.tensor_tensor(WM[:, :, :, :].rearrange("p g h q -> p (g h) q"),
                                        MI[:, :].rearrange("p (n q) -> p n q", q=WB),
                                        bc(k["wmask"][:, :], 1, H * P // QB), ALU.mult).then_inc(s["w_masked"], 1)

            def normalise(at, first):
                dve.wait_ge(s["xtt_ready"], at.count(1, 1))
                v = MI[:, :].rearrange("p (n c) -> p n c", c=32)
                nc.vector.reciprocal(RD[:, :], v[:, :, HD]).then_inc(s["rd"], 1)
                dve.wait_ge(s["rd"], at.count(1, 1))
                if since_start(first, at, 2):
                    dve.wait_ge(xo_out[at.c % 2], at.even(1) * 16)
                xn = XN[at.c % 2][:, :].rearrange("p (a g d) -> p g a d", a=NQ4, d=HD)
                nc.vector.tensor_tensor(xn, MI[:, :].rearrange("p (g a c) -> p g a c", g=NQ4, a=NQ4)[:, :, :, 0:HD],
                                        bc(RD[:, :].rearrange("p (g a) -> p g a", g=NQ4), 3, HD), ALU.mult).then_inc(s["norm"], 1)

            row_max(At(0, 0), range(H))
            guard_parts(At(0, 0))
            row_max(At(0, 1), range(H))

            def unit(at, first, last):
                before = at.plus(-1)
                if exists(at, first, last, 1):
                    guard_parts(at.plus(1))
                for c in range(SUB):
                    if exists(at, first, last, 2):
                        row_max(at.plus(2), range(2 * c, 2 * c + 2))
                    if exists(at, first, last, -1):
                        if c == 1:
                            keep_values(before, first)
                        if c == 4:
                            normalise(before, first)

            run(dve, unit)
            end = At(U // PER - 1, PER - 1)
            keep_values(end, False)
            normalise(end, False)


def stage_output(nc, m, k, d):
    xa, x, x1, xn, fin = (m.sb(f"c_{n}", [P, T, E]) for n in ("xa", "x", "x1", "xn", "fin"))
    aT, xnT = m.sb("c_aT", [P, S]), m.sb("c_xnT", [P, S])
    sg, hh = m.sb("c_sg", [P, FC, S]), m.sb("c_hh", [P, FC, S])
    tmp = {"st": m.sb("c_st", [P, T, 6]), "mv": m.sb("c_mv", [P, T, 2]), "std": m.sb("c_std", [P, T]),
           "rstd": m.sb("c_rstd", [P, T]), "gap": m.sb("c_gap", [P, 1])}
    pT, py = m.ps("c_pt", [P, S]), m.ps("c_py", [P, S])
    pg, pu = m.ps("c_pg", [P, FC, S]), m.ps("c_pu", [P, FC, S])
    names = ("in", "aT", "aTs", "y", "x1", "var", "std", "xn", "xT", "xTs", "gate", "up", "silu", "hid", "down", "fin",
             "out", "xb", "dv")
    s = {n: m.sem("c_s_" + n) for n in names}
    NCH = 2
    with nc.Block() as block:
        @block.sync
        def _(sp):
            def batch(b):
                wait_past(sp, s["x1"], b)
                wait_past(sp, s["aT"], b)
                sp.dma_start(xa[:, :, :], d["xo"][bass.ds(b * T, T)].rearrange("t p e -> p t e")).then_inc(s["in"], 16)
                sp.dma_start(x[:, :, :], d["x"][bass.ds(b, 1)].rearrange("o (t p) e -> p (o t) e", p=P)).then_inc(s["in"], 16)
                sp.wait_ge(s["fin"], b + 1)
                sp.dma_start(d["out"][bass.ds(b, 1)].rearrange("o (t p) e -> p (o t) e", p=P), fin[:, :, :]).then_inc(s["out"], 16)

            batches(sp, batch)
            sp.wait_ge(s["out"], 16 * B)

        @block.gpsimd
        def _(pool):
            def batch(b):
                pool.wait_ge(s["in"], 32 * b + 32)
                nc.gpsimd.tensor_tensor(x[:, :, :], x[:, :, :], bc(k["bo"][:, :], 1, T), ALU.add).then_inc(s["xb"], 1)

            batches(pool, batch)

        @block.tensor
        def _(pe):
            def batch(b):
                pe.wait_ge(s["in"], 32 * b + 32)
                wait_past(pe, s["xTs"], b)
                for t in range(T):
                    ins = nc.tensor.transpose(pT[:, t * P:(t + 1) * P], xa[:, t, :], k["ident"][:, :])
                ins.then_inc(s["aT"], 1)
                pe.wait_ge(s["aTs"], b + 1)
                wait_past(pe, s["fin"], b)
                for t in range(T):
                    ins = nc.tensor.matmul(py[:, t * P:(t + 1) * P], aT[:, t * P:(t + 1) * P], k["wo"][:, :], start=True, stop=True)
                ins.then_inc(s["y"], 1)
                pe.wait_ge(s["xn"], b + 1)
                for t in range(T):
                    ins = nc.tensor.transpose(pT[:, t * P:(t + 1) * P], xn[:, t, :], k["ident"][:, :])
                ins.then_inc(s["xT"], 1)
                pe.wait_ge(s["xTs"], b + 1)
                wait_past(pe, s["hid"], FC * b)
                for c in range(FC):
                    nc.tensor.matmul(pg[:, c, :], k["wg"][:, c * P:(c + 1) * P], xnT[:, :], start=True, stop=True).then_inc(s["gate"], 1)
                    nc.tensor.matmul(pu[:, c, :], k["wu"][:, c * P:(c + 1) * P], xnT[:, :], start=True, stop=True).then_inc(s["up"], 1)
                pe.wait_ge(s["hid"], FC * b + FC)
                pe.wait_ge(s["x1"], b + 1)
                for t in range(T):
                    for c in range(FC):
                        ins = nc.tensor.matmul(py[:, t * P:(t + 1) * P], hh[:, c, t * P:(t + 1) * P], k["wd"][:, c, :],
                                               start=c == 0, stop=c == FC - 1)
                ins.then_inc(s["down"], 1)

            batches(pe, batch)

        @block.scalar
        def _(act):
            def batch(b):
                act.wait_ge(s["aT"], b + 1)
                nc.scalar.copy(aT[:, :], pT[:, :]).then_inc(s["aTs"], 1)
                act.wait_ge(s["var"], b + 1)
                nc.scalar.activation(tmp["std"][:, :], tmp["mv"][:, :, 1], ACT.Sqrt, bias=k["eps"][:, 0:1]).then_inc(s["std"], 1)
                act.wait_ge(s["xT"], b + 1)
                nc.scalar.copy(xnT[:, :], pT[:, :]).then_inc(s["xTs"], 1)
                for c in range(FC):
                    act.wait_ge(s["gate"], FC * b + c + 1)
                    nc.scalar.activation(sg[:, c, :], pg[:, c, :], ACT.Silu).then_inc(s["silu"], 1)

            batches(act, batch)

        @block.vector
        def _(dve):
            def batch(b):
                n = 0

                def chain(ins):
                    nonlocal n
                    n += 1
                    ins.then_inc(s["dv"], 1)
                    dve.wait_ge(s["dv"], b * NCH + n)

                dve.wait_ge(s["y"], b + 1)
                dve.wait_ge(s["xb"], b + 1)
                nc.vector.tensor_tensor(x1[:, :, :], py[:, :].rearrange("p (t e) -> p t e", t=T), x[:, :, :], ALU.add).then_inc(s["x1"], 1)
                dve.wait_ge(s["x1"], b + 1)
                layernorm_vector(nc, dve, x1, xn, tmp, chain, s["var"], s["std"], b).then_inc(s["xn"], 1)
                for c in range(FC):
                    dve.wait_ge(s["silu"], FC * b + c + 1)
                    dve.wait_ge(s["up"], FC * b + c + 1)
                    nc.vector.tensor_tensor(hh[:, c, :], sg[:, c, :], pu[:, c, :], ALU.mult).then_inc(s["hid"], 1)
                dve.wait_ge(s["down"], b + 1)
                wait_past(dve, s["out"], 16 * b)
                nc.vector.tensor_tensor(fin[:, :, :], py[:, :].rearrange("p (t e) -> p t e", t=T), x1[:, :, :], ALU.add).then_inc(s["fin"], 1)

            batches(dve, batch)


def program(nc, d):
    for name, shape, dt in (("qop", (B, SLOTS, P, S), BF16), ("kop", (B, SLOTS, P, S), BF16),
                            ("qf", (B, P, S), F32), ("vg", (B, P, VGW), F32), ("xo", (U, P, E), F32),
                            ("gt", (2, 6 * H, P), BF16)):
        d[name] = nc.dram_tensor("scratch_" + name, shape, dt, kind="Internal").ap()
    with ExitStack() as keep:
        m = Memory(nc, keep)
        k = {"ident": m.sb("ident", [P, P]), "qmask": m.sb("qmask", [P, QB]), "wmask": m.sb("wmask", [P, WB]),
             "red": m.sb("red", [P, NQ4, V16]), "zlo": m.sb("zlo", [P, ZLO_W]), "zhi": m.sb("zhi", [P, ZHI_W]),
             "tvd": m.sb("tvd", [P, P * HD]), "tvm": m.sb("tvm", [P, REL * HD]), "tvp": m.sb("tvp", [P, REL * HD]),
             "wq": m.sb("wq", [P, P]), "wk": m.sb("wk", [P, P]), "wv": m.sb("wv", [P, P]), "wo": m.sb("wo", [P, P]),
             "bq": m.sb("bq", [P, 1]), "bk0": m.sb("bk0", [P, 1]), "relend": m.sb("relend", [P, H]),
             "bv2": m.sb("bv2", [P, 2, P]), "bo": m.sb("bo", [P, P]), "relbd": m.sb("relbd", [P, 2, H * REL], BF16),
             "wg": m.sb("wg", [P, F]), "wu": m.sb("wu", [P, F]), "wd": m.sb("wd", [P, FC, P]), "eps": m.sb("eps", [P, 1])}
        for stage in (setup_constants, stage_project, stage_attend, stage_output):
            with ExitStack() as ctx:
                stage(nc, Memory(nc, ctx), k, d)


def kernel(**inputs):
    import concourse.bacc as _bacc
    from concourse.bass_utils import run_bass_kernel_spmd as _run

    a = {n.removeprefix("L0_"): np.asarray(v) for n, v in inputs.items()}
    rel_k, rel_v = a["attn_rel_k"], a["attn_rel_v"]

    def by_d(w):
        return w.reshape(H, HD, *w.shape[1:]).swapaxes(0, 1).reshape(P, *w.shape[1:])

    clipped = np.clip(np.arange(-EXT_0, EXT_0 + 1), -REL, REL) + REL
    arrays = {
        "x": a["attn_hidden_states"],
        "wq": by_d(a["attn_Wq"]).T, "wk": by_d(a["attn_Wk"]).T, "wv": a["attn_Wv"].T, "wo": a["attn_Wo"].T,
        "bq": by_d(a["attn_bq"])[:, None], "bk": by_d(a["attn_bk"])[:, None],
        "bv": a["attn_bv"][None, :], "bo": a["attn_bo"][None, :],
        "rkh": np.repeat(rel_k.T, H, axis=0),
        "rkj": np.tile(rel_k[[0, NREL - 1]].T, (QB, 1)),
        "rkx": rel_k[clipped].T, "rvx": rel_v[clipped], "rv": rel_v,
        "wg": a["ffn_w_gate"].T, "wu": a["ffn_w_up"].T, "wd": a["ffn_w_down"].T,
    }
    arrays = {"in_" + n: np.ascontiguousarray(v) for n, v in arrays.items()}
    nc = _bacc.Bacc("TRN2", target_bir_lowering=False, num_devices=1)
    d = {n[3:]: nc.dram_tensor(n, v.shape, mybir.dt.from_np(v.dtype), kind="ExternalInput").ap() for n, v in arrays.items()}
    d["out"] = nc.dram_tensor("out", (B, S, E), F32, kind="ExternalOutput").ap()
    program(nc, d)
    r = _run(nc, [arrays], core_ids=[0])
    return r.results[0]["out"]
```

```python
from contextlib import ExitStack

import numpy as np

import concourse.bass as bass
from concourse import mybir

F32 = mybir.dt.float32
BF16 = mybir.dt.bfloat16
I32 = mybir.dt.int32
ALU = mybir.AluOpType
ACT = mybir.ActivationFunctionType
AX_X = mybir.AxisListType.X

P = 128
B, S, E = 16, 512, 128
H, HD = 16, 8
REL = 20
NREL = 2 * REL + 1
T = S // P
U = B * T
F = 384
FC = F // P
EPS = 1e-5

SLOTS = 6
K_SLOT = {0: (0, 3, 5), 1: (1, 4), 2: (2,)}
Q_SLOT = {0: (0, 1, 2), 1: (3, 4), 2: (5,)}
OPR = SLOTS * HD
GROW = 96
DROW = GROW + 3
ROWS = DROW + 3

HG = 8
NG = H // HG
SUB = T * NG
QB = 16
WB = 8
WR = P // (WB * HD)
CW = -(-REL // WB) * WB
V16 = 16
NQ4 = 4

ZLO_W, ZLO_0 = 272, 144
ZHI_W, ZHI_0 = 144, -16
EXT_0 = 176
EXT = 2 * EXT_0 + 1
VW = 2 * T * H * V16
VGW = VW + 4 * T * H


def bc(ap, axis, n):
    ap = ap.unsqueeze(axis)
    shape = list(ap.shape)
    shape[axis] = n
    return ap.to_broadcast(shape)


class At:

    def __init__(self, it, c, per, total):
        self.it, self.c, self.per, self.total = it, c, per, total
        self.fixed = isinstance(it, int)

    def plus(self, n):
        return At(self.it, self.c + n, self.per, self.total)

    def count(self, each=1, extra=0):
        return self.it * (self.per * each) + (self.c * each + extra)

    def even(self, n):
        return self.it * (self.per // (2 * n)) + self.c // (2 * n)

    def exists(self):
        return not self.fixed or 0 <= self.it * self.per + self.c < self.total

    def since(self, n):
        return not self.fixed or self.it * self.per + self.c >= n


def run(eng, step, per, total):
    for c in range(per):
        step(At(0, c, per, total))
    with eng.Fori(1, total // per - 1) as it:
        for c in range(per):
            step(At(it, c, per, total))
    for c in range(per):
        step(At(total // per - 1, c, per, total))


class Memory:

    def __init__(self, nc, ctx):
        self.nc, self.ctx = nc, ctx

    def sb(self, name, shape, dt=F32):
        return self.ctx.enter_context(self.nc.sbuf_tensor(name, shape, dt))

    def ps(self, name, shape, dt=F32):
        return self.ctx.enter_context(self.nc.psum_tensor(name, shape, dt))

    def sem(self, name):
        return self.ctx.enter_context(self.nc.semaphore(name))


def setup_constants(nc, m, k, d):
    s_ld, s_id, s_z, s_v = m.sem("su_loaded"), m.sem("su_pool"), m.sem("su_zero"), m.sem("su_vector")
    ones = m.sb("su_ones", [P, P])
    wgi = m.sb("su_wgi", [P, F], I32)
    wui = m.sb("su_wui", [P, F], I32)
    wdi = m.sb("su_wdi", [P, FC, P], I32)
    bkc = m.sb("su_bk", [P, 1])
    rkc, rkj = m.sb("su_rkc", [P, NREL]), m.sb("su_rkj", [P, 2])
    bvb, rvb = m.sb("su_bvb", [P, P]), m.sb("su_rvb", [P, 2, HD])
    rkd = m.sb("su_rkd", [P, NREL])
    hm = m.sb("su_hm", [P, H])
    loads = []

    def toeplitz_k(dst, width, first):
        for jr in range(QB):
            src = d["rkx"][:, EXT_0 + first + jr:EXT_0 + first + jr + width]
            loads.append((dst[jr * HD:(jr + 1) * HD, :], src))

    def toeplitz_v(dst, nq, first):
        src = bass.AP(d["rvx"].tensor, (EXT_0 + first) * HD, [[HD, P], [1, nq * HD]])
        loads.append((dst, src))

    toeplitz_k(k["zlo"][:, :], ZLO_W, 1 - QB - ZLO_0)
    toeplitz_k(k["zhi"][:, :], ZHI_W, 1 - QB - ZHI_0)
    toeplitz_v(k["tvd"][:, :], P, 1 - P)
    toeplitz_v(k["tvm"][:, :], CW, 1 - P - CW)
    toeplitz_v(k["tvp"][:, :], CW, 1)
    for n in ("wq", "wk", "wv", "wo"):
        loads.append((k[n][:, :], d[n]))
    loads += [(wgi[:, :], d["wg"]), (wui[:, :], d["wu"]), (wdi[:, :, :], d["wd"].rearrange("(c p) e -> p c e", p=P)),
              (k["bq"][:, :], d["bq"]), (bkc[:, :], d["bk"]), (rkc[:, :], d["rkh"]), (rkj[:, :], d["rkj"]),
              (bvb[:, :], d["bv"].to_broadcast([P, P])), (k["bo"][:, :], d["bo"].to_broadcast([P, P])),
              (rvb[:, 0, :], d["rv"][0:1, :].to_broadcast([P, HD])),
              (rvb[:, 1, :], d["rv"][NREL - 1:NREL, :].to_broadcast([P, HD]))]
    with nc.Block() as block:
        @block.sync
        def _(sp):
            for dst, src in loads:
                sp.dma_start(dst, src).then_inc(s_ld, 16)

        @block.gpsimd
        def _(pool):
            n = 0

            def link(ins):
                nonlocal n
                n += 1
                ins.then_inc(s_id, 1)
                pool.wait_ge(s_id, n)

            link(nc.gpsimd.memset(ones[:, :], 1.0))
            link(nc.gpsimd.memset(k["ident"][:, :], 0.0))
            link(nc.gpsimd.affine_select(out=k["ident"][:, :], in_=k["ident"][:, :], compare_op=ALU.not_equal, fill=1.0,
                                         base=0, pattern=[[-1, P]], channel_multiplier=1))
            link(nc.gpsimd.affine_select(out=k["qmask"][:, :], in_=ones[:, 0:QB], compare_op=ALU.is_ge, fill=0.0,
                                         base=-HD * (QB - 1), pattern=[[HD, QB]], channel_multiplier=1))
            link(nc.gpsimd.affine_select(out=k["qmask"][:, :], in_=k["qmask"][:, :], compare_op=ALU.is_ge, fill=0.0,
                                         base=HD * QB - 1, pattern=[[-HD, QB]], channel_multiplier=-1))
            for b in range(WR):
                w = k["wmask"][b * WB * HD:(b + 1) * WB * HD, :]
                link(nc.gpsimd.affine_select(out=w, in_=ones[b * WB * HD:(b + 1) * WB * HD, 0:WB], compare_op=ALU.is_ge, fill=0.0,
                                             base=-HD * (WB - 1), pattern=[[HD, WB]], channel_multiplier=1))
                link(nc.gpsimd.affine_select(out=w, in_=w, compare_op=ALU.is_ge, fill=0.0,
                                             base=HD * WB - 1, pattern=[[-HD, WB]], channel_multiplier=-1))
            link(nc.gpsimd.memset(k["red"][:, :, :], 0.0))

        @block.vector
        def _(dve):
            n = 0

            def link(ins):
                nonlocal n
                n += 1
                ins.then_inc(s_v, 1)
                dve.wait_ge(s_v, n)

            dve.wait_ge(s_ld, 16 * len(loads))
            dve.wait_ge(s_id, 5 + 2 * WR + 1)
            link(nc.vector.tensor_scalar(k["zlo"][:, :], k["zlo"][:, :], rkj[:, 0:1], None, ALU.subtract))
            link(nc.vector.tensor_scalar(k["zhi"][:, :], k["zhi"][:, :], rkj[:, 1:2], None, ALU.subtract))
            for name, nq, side in (("tvd", P, 0), ("tvm", CW, 0), ("tvp", CW, 1)):
                v = k[name][:, :].rearrange("p (q d) -> p q d", d=HD)
                link(nc.vector.tensor_tensor(v, v, bc(rvb[:, side, :], 1, nq), ALU.subtract))
            link(nc.vector.tensor_tensor(k["bk0"][:, :], bkc[:, :], rkc[:, 0:1], ALU.add))
            for side in range(2):
                link(nc.vector.tensor_tensor(k["bv2"][:, side, :].rearrange("p (h d) -> p h d", d=HD),
                                             bvb[:, :].rearrange("p (h d) -> p h d", d=HD),
                                             bc(rvb[:, side, :], 1, H), ALU.add))
            link(nc.vector.tensor_reduce(hm[:, :], k["ident"][:, :].rearrange("p (d h) -> p h d", h=H), AX_X, ALU.add))
            link(nc.vector.tensor_scalar(rkd[:, :], rkc[:, :], rkc[:, 0:1], None, ALU.subtract))
            link(nc.vector.tensor_scalar(k["relend"][:, :], hm[:, :], rkd[:, NREL - 1:NREL], None, ALU.mult))
            for i in range(2):
                link(nc.vector.tensor_tensor(k["relbd"][:, i, :].rearrange("p (h r) -> p h r", h=H),
                                             bc(rkd[:, 1 + REL * i:1 + REL * (i + 1)], 1, H),
                                             bc(hm[:, :], 2, REL), ALU.mult))
            link(nc.vector.tensor_reduce(k["red"][:, :, 0:HD],
                                         k["ident"][:, :].rearrange("p (b j d) -> p b d j", b=WR, d=HD), AX_X, ALU.add))
            for dst, src in ((k["wg"][:, :], wgi[:, :]), (k["wu"][:, :], wui[:, :]), (k["wd"][:, :, :], wdi[:, :, :])):
                link(nc.vector.tensor_copy(dst, src))
                link(nc.vector.tensor_scalar(dst, dst, float(np.float32(1.0 / 127.0)), None, ALU.mult))
            link(nc.vector.memset(k["eps"][:, :], EPS))


def layernorm_statistics(nc, x, tmp, link, s_var):
    for t in range(T):
        ins = nc.vector.bn_stats(tmp["st"][:, t, :], x[:, t, :])
    link(ins)
    nc.vector.memset(tmp["gap"][:, :], 0.0)
    for t in range(T):
        ins = nc.vector.bn_aggr(tmp["mv"][:, t, :], tmp["st"][:, t, :])
    ins.then_inc(s_var, 1)


def layernorm_rows(nc, x, xn, tmp, link):
    link(nc.vector.reciprocal(tmp["rstd"][:, :], tmp["std"][:, :]))
    for t in range(T):
        ins = nc.vector.tensor_scalar(xn[:, t, :], x[:, t, :], tmp["mv"][:, t, 0:1], tmp["rstd"][:, t:t + 1],
                                      ALU.subtract, ALU.mult)
    return ins


def stage_project(nc, m, k, d):
    X = [m.sb(f"a_x{p}", [P, T, E]) for p in range(2)]
    xn = m.sb("a_xn", [P, T, E])
    xnT = m.sb("a_xnT", [P, S])
    QF = [m.sb(f"a_qf{p}", [P, 2, S]) for p in range(2)]
    PARTS = [m.sb(f"a_parts{p}", [P, 2, 3, S], BF16) for p in range(2)]
    VT = [m.sb(f"a_vt{p}", [P, VGW]) for p in range(2)]
    qr, kr = m.sb("a_qr", [P, S]), m.sb("a_kr", [P, S])
    db, dr = m.sb("a_db", [P, 3, T * H], BF16), m.sb("a_dr", [P, T * H])
    gr = m.sb("a_gr", [P, 2, T, H])
    tmp = {"st": m.sb("a_st", [P, T, 6]), "mv": m.sb("a_mv", [P, T, 2]), "std": m.sb("a_std", [P, T]),
           "rstd": m.sb("a_rstd", [P, T]), "gap": m.sb("a_gap", [P, 1])}
    pT, pq, pk, pv = (m.ps(f"a_p{n}", [P, S]) for n in "tqkv")
    pd = m.ps("a_pd", [P, T * H])
    pr = [m.ps(f"a_pr{n}", [P, S]) for n in range(2)]
    names = ("x_in0", "x_in1", "var", "std", "xn", "xT", "xTs", "proj", "fevac", "qsplit", "ksplit", "vevac", "ends",
             "dsplit", "rel", "relmax", "vdone", "out0", "out1", "dv", "pl", "vinit")
    s = {n: m.sem("a_s_" + n) for n in names}
    x_in, out = ([s[f"{n}{p}"] for p in range(2)] for n in ("x_in", "out"))
    NLINK = 1 + 1 + 2 + 3 + 1
    NOUT = 3 + 4 + 1 + 1

    def at0(c):
        return At(0, c, 2, B)

    with nc.Block() as block:
        @block.sync
        def _(sp):
            def load_x(at):
                sp.dma_start(X[at.c % 2][:, :, :],
                             d["x"][bass.ds(at.count(), 1)].rearrange("o (t p) e -> p (o t) e", p=P)).then_inc(x_in[at.c % 2], 16)

            load_x(at0(0))
            load_x(at0(1))

            def step(at):
                p = at.c % 2
                sp.wait_ge(s["xn"], at.count(1, 1))
                if at.plus(2).exists():
                    load_x(at.plus(2))
                dsts = [d[n][bass.ds(at.count(), 1)].rearrange("o s p t -> p (o s) t") for n in ("qop", "kop")]
                sp.wait_ge(s["qsplit"], at.count(1, 1))
                for part, slots in Q_SLOT.items():
                    sp.dma_start(dsts[0][:, slots[0]:slots[-1] + 1, :],
                                 bc(PARTS[p][:, 0, part, :], 1, len(slots))).then_inc(out[p], 16)
                sp.dma_start(d["qf"][bass.ds(at.count(), 1)].rearrange("o p t -> p (o t)"), QF[p][:, 0, :]).then_inc(out[p], 16)
                sp.wait_ge(s["ksplit"], at.count(1, 1))
                for part, slots in ((0, (0, 3)), (0, (5,)), (1, (1, 4)), (2, (2,))):
                    sp.dma_start(dsts[1][:, slots[0]:slots[-1] + 1:3, :],
                                 bc(PARTS[p][:, 1, part, :], 1, len(slots))).then_inc(out[p], 16)
                sp.wait_ge(s["vdone"], at.count(1, 1))
                sp.dma_start(d["vg"][bass.ds(at.count(), 1)].rearrange("o p t -> p (o t)"), VT[p][:, :]).then_inc(out[p], 16)

            run(sp, step, 2, B)
            for p in range(2):
                sp.wait_ge(out[p], 16 * NOUT * B // 2)

        @block.tensor
        def _(pe):
            def transposes(at):
                pe.wait_ge(s["xn"], at.count(1, 1))
                if at.since(1):
                    pe.wait_ge(s["xTs"], at.count())
                for t in range(T):
                    ins = nc.tensor.transpose(pT[:, t * P:(t + 1) * P], xn[:, t, :], k["ident"][:, :])
                ins.then_inc(s["xT"], 1)

            def projections(at):
                pe.wait_ge(s["xTs"], at.count(1, 1))
                if at.since(1):
                    pe.wait_ge(s["fevac"], at.count())
                    pe.wait_ge(s["vevac"], at.count())
                nc.tensor.matmul(pq[:, :], k["wq"][:, :], xnT[:, :], start=True, stop=True)
                nc.tensor.matmul(pk[:, :], k["wk"][:, :], xnT[:, :], start=True, stop=True)
                for t in range(T):
                    ins = nc.tensor.matmul(pv[:, t * P:(t + 1) * P], xnT[:, t * P:(t + 1) * P], k["wv"][:, :],
                                           start=True, stop=True)
                ins.then_inc(s["proj"], 1)

            def relative_terms(at):
                p = at.c % 2
                pe.wait_ge(s["fevac"], at.count(1, 1))
                if at.since(1):
                    pe.wait_ge(s["dsplit"], at.count())
                for t in range(T):
                    ins = nc.tensor.matmul(pd[:, t * H:(t + 1) * H], QF[p][:, 0, t * P:(t + 1) * P], k["relend"][:, :],
                                           start=True, stop=True)
                ins.then_inc(s["ends"], 1)
                for t in range(T):
                    if t or at.since(1):
                        pe.wait_ge(s["relmax"], at.count(T, t))
                    for i in range(2):
                        ins = nc.tensor.matmul(pr[i][:, 0:H * REL], PARTS[p][:, 0, 0, t * P:(t + 1) * P],
                                               k["relbd"][:, i, :], start=True, stop=True)
                    ins.then_inc(s["rel"], 1)

            transposes(at0(0))
            projections(at0(0))

            def step(at):
                if at.plus(1).exists():
                    transposes(at.plus(1))
                    projections(at.plus(1))
                relative_terms(at)

            run(pe, step, 2, B)

        @block.scalar
        def _(act):
            def rows(at):
                p = at.c % 2
                act.wait_ge(s["var"], at.count(1, 1))
                nc.scalar.activation(tmp["std"][:, :], tmp["mv"][:, :, 1], ACT.Sqrt, bias=k["eps"][:, 0:1]).then_inc(s["std"], 1)
                act.wait_ge(s["xT"], at.count(1, 1))
                if at.since(1):
                    act.wait_ge(s["proj"], at.count())
                nc.scalar.copy(xnT[:, :], pT[:, :]).then_inc(s["xTs"], 1)
                act.wait_ge(s["proj"], at.count(1, 1))
                if at.since(2):
                    act.wait_ge(out[p], at.even(1) * (16 * NOUT))
                nc.scalar.activation(PARTS[p][:, 0, 0, :], pq[:, :], ACT.Identity, bias=k["bq"][:, 0:1])
                nc.scalar.activation(QF[p][:, 0, :], pq[:, :], ACT.Identity, bias=k["bq"][:, 0:1])
                nc.scalar.activation(PARTS[p][:, 1, 0, :], pk[:, :], ACT.Identity, bias=k["bk0"][:, 0:1])
                nc.scalar.activation(QF[p][:, 1, :], pk[:, :], ACT.Identity, bias=k["bk0"][:, 0:1]).then_inc(s["fevac"], 1)

            rows(at0(0))

            def step(at):
                if at.plus(1).exists():
                    rows(at.plus(1))

            run(act, step, 2, B)

        @block.gpsimd
        def _(pool):
            def step(at):
                p = at.c % 2
                pool.wait_ge(s["fevac"], at.count(1, 1))
                if at.since(1):
                    pool.wait_ge(s["ksplit"], at.count())
                nc.gpsimd.tensor_tensor(kr[:, :], QF[p][:, 1, :], PARTS[p][:, 1, 0, :], ALU.subtract)
                nc.gpsimd.tensor_tensor(PARTS[p][:, 1, 1, :], QF[p][:, 1, :], PARTS[p][:, 1, 0, :], ALU.subtract).then_inc(s["pl"], 1)
                pool.wait_ge(s["pl"], at.count(1, 1))
                nc.gpsimd.tensor_tensor(PARTS[p][:, 1, 2, :], kr[:, :], PARTS[p][:, 1, 1, :], ALU.subtract).then_inc(s["ksplit"], 1)

            run(pool, step, 2, B)

        @block.vector
        def _(dve):
            for p in range(2):
                nc.vector.memset(VT[p][:, 0:VW], 0.0).then_inc(s["vinit"], 1)
            dve.wait_ge(s["vinit"], 2)
            for p in range(2):
                nc.vector.memset(VT[p][:, 0:VW].rearrange("p (n c) -> p n c", c=V16)[:, :, HD:HD + 1], 1.0).then_inc(s["vinit"], 1)
            dve.wait_ge(s["vinit"], 4)

            def linker(at, done):
                def link(ins):
                    nonlocal done
                    done += 1
                    ins.then_inc(s["dv"], 1)
                    dve.wait_ge(s["dv"], at.count(NLINK, done))
                return link

            def normalise(at, link):
                p = at.c % 2
                dve.wait_ge(x_in[p], at.even(1) * 16 + 16)
                layernorm_statistics(nc, X[p], tmp, link, s["var"])
                dve.wait_ge(s["std"], at.count(1, 1))
                if at.since(1):
                    dve.wait_ge(s["xT"], at.count())
                layernorm_rows(nc, X[p], xn, tmp, link).then_inc(s["xn"], 1)

            normalise(at0(0), linker(at0(0), 0))

            def step(at):
                p = at.c % 2
                if at.plus(1).exists():
                    normalise(at.plus(1), linker(at, 2))
                    link = linker(at, 2 + 2)
                else:
                    link = linker(at, 2)
                dve.wait_ge(s["fevac"], at.count(1, 1))
                link(nc.vector.tensor_tensor(qr[:, :], QF[p][:, 0, :], PARTS[p][:, 0, 0, :], ALU.subtract))
                link(nc.vector.tensor_copy(PARTS[p][:, 0, 1, :], qr[:, :]))
                nc.vector.tensor_tensor(PARTS[p][:, 0, 2, :], qr[:, :], PARTS[p][:, 0, 1, :], ALU.subtract).then_inc(s["qsplit"], 1)
                for side in range(2):
                    o = VT[p][:, side * VW // 2:(side + 1) * VW // 2].rearrange("p (t h c) -> p t h c", t=T, h=H)
                    ins = nc.vector.tensor_tensor(o[:, :, :, 0:HD], pv[:, :].rearrange("p (t h d) -> p t h d", t=T, h=H),
                                                  bc(k["bv2"][:, side, :].rearrange("p (h d) -> p h d", h=H), 1, T), ALU.add)
                ins.then_inc(s["vevac"], 1)
                dve.wait_ge(s["ends"], at.count(1, 1))
                link(nc.vector.tensor_copy(db[:, 0, :], pd[:, :]))
                nc.vector.tensor_tensor(dr[:, :], pd[:, :], db[:, 0, :], ALU.subtract).then_inc(s["dsplit"], 1)
                dve.wait_ge(s["dsplit"], at.count(1, 1))
                link(nc.vector.tensor_copy(db[:, 1, :], dr[:, :]))
                link(nc.vector.tensor_tensor(db[:, 2, :], dr[:, :], db[:, 1, :], ALU.subtract))
                nc.vector.tensor_copy(VT[p][:, VW + T * H:VGW], db[:, :, :].rearrange("p c n -> p (c n)"))
                for t in range(T):
                    dve.wait_ge(s["rel"], at.count(T, t + 1))
                    for i in range(2):
                        ins = nc.vector.reduce_max(gr[:, i, t, :], pr[i][:, 0:H * REL].rearrange("p (h r) -> p h r", h=H), AX_X)
                    ins.then_inc(s["relmax"], 1)
                dve.wait_ge(s["relmax"], at.count(T, T))
                link(nc.vector.tensor_tensor(gr[:, 0, :, :], gr[:, 0, :, :], gr[:, 1, :, :], ALU.max))
                nc.vector.tensor_scalar(VT[p][:, VW:VW + T * H].rearrange("p (t h) -> p t h", t=T), gr[:, 0, :, :], 0.0, None,
                                        ALU.max).then_inc(s["vdone"], 1)

            run(dve, step, 2, B)


def stage_attend(nc, m, k, d):
    K = [m.sb(f"b_k{p}", [P, H, S], BF16) for p in range(2)]
    Q = [m.sb(f"b_q{p}", [P, H, S], BF16) for p in range(2)]
    VG = [m.sb(f"b_v{p}", [P, VGW]) for p in range(2)]
    QD = [m.sb(f"b_qd{p}", [P, H, P]) for p in range(2)]
    PR = [m.sb(f"b_p{p}", [P, T, H, P]) for p in range(2)]
    WM = m.sb("b_wm", [P, 2, P // (2 * WR * WB), H, WB])
    XT = m.sb("b_xt", [P, NQ4 * P])
    XN = [m.sb(f"b_xn{p}", [P, E]) for p in range(2)]
    RD = m.sb("b_rd", [P, H])
    MX = [m.sb(f"b_mx{p}", [P, H]) for p in range(2)]
    nm, r1, r2 = (m.sb(f"b_{n}", [P, H]) for n in ("nm", "r1", "r2"))
    NP = m.sb("b_np", [P, 6, H], BF16)
    MT = m.sb("b_mt", [6 * H, P], BF16)
    idb = m.sb("b_idb", [P, P], BF16)
    SC = [m.ps(f"b_s{p}", [P, 2, S]) for p in range(2)]
    PA = [m.ps(f"b_a{p}", [P, S]) for p in range(2)]
    PV = m.ps("b_pv", [P, NQ4 * P])
    MI = m.ps("b_mi", [P, S])
    names = ("init", "a_ready", "a_used", "s_ready", "p_ready", "w_ready", "w_masked", "pv_ready", "xt_ready", "rd",
             "mp_ready", "mt_ready", "mt_copied", "xtt_ready", "norm", "m_out", "m_in", "xo_out0", "xo_out1",
             "qd_masked", "dv", "kq_in0", "kq_in1", "v_in0", "v_in1", "qd_in0", "qd_in1")
    s = {n: m.sem("b_s_" + n) for n in names}
    kq_in, v_in, qd_in, xo_out = ([s[f"{n}{p}"] for p in range(2)] for n in ("kq_in", "v_in", "qd_in", "xo_out"))
    NKQ, NQD = 2, QB
    MCH = 6
    SCALE = float(1.0 / np.sqrt(np.float32(HD)))

    PER = 2 * T

    def at0(c):
        return At(0, c, PER, U)

    def window(t, i):
        return abs(t - i) <= 1

    with nc.Block() as block:
        @block.sync
        def _(sp):
            def load_kq(at):
                p = (at.c // T) % 2
                dram = at.it * 2 + at.c // T
                for name, dst in (("kop", K[p]), ("qop", Q[p])):
                    sp.dma_start(dst[0:OPR, :, :], d[name][bass.ds(dram, 1)].rearrange("o s (d h) t -> (o s d) h t", h=H))\
                        .then_inc(kq_in[p], 16)

            def load_v(at):
                p = (at.c // T) % 2
                sp.dma_start(VG[p][:, :], d["vg"][bass.ds(at.it * 2 + at.c // T, 1)].rearrange("o p c -> (o p) c")).then_inc(v_in[p], 16)

            def load_qd(at):
                p = at.c % 2
                i = at.c % T
                src = d["qf"][bass.ds(at.it * 2 + at.c // T, 1), :, i * P:(i + 1) * P].rearrange("o (d h) t -> (o d) h t", h=H)
                for jr in range(QB):
                    sp.dma_start(QD[p][jr * HD:(jr + 1) * HD, :, :], src).then_inc(qd_in[p], 16)

            def guard_rows(at):
                sp.wait_ge(s["mt_copied"], at.count(1, 1))
                sp.dma_start(d["gt"][at.c % 2], MT[:, :]).then_inc(s["m_out"], 16)
                sp.wait_ge(s["m_out"], at.count(16, 16))
                p, i = (at.c // T) % 2, at.c % T
                sp.dma_start(Q[p][GROW:ROWS, :, i * P:(i + 1) * P], d["gt"][at.c % 2].rearrange("(c h) q -> c h q", h=H))\
                    .then_inc(s["m_in"], 16)

            sp.wait_ge(s["init"], 4)
            load_kq(at0(0))
            load_v(at0(0))
            load_qd(at0(0))
            load_kq(at0(T))
            load_v(at0(T))
            guard_rows(at0(0))

            def unit(at):
                if at.since(1):
                    sp.wait_ge(s["s_ready"], at.count(SUB))
                if at.plus(1).exists():
                    load_qd(at.plus(1))
                if at.c % T == 0 and at.since(T) and at.plus(T).exists():
                    load_kq(at.plus(T))
                    sp.wait_ge(s["w_ready"], at.count(2))
                    load_v(at.plus(T))
                if at.since(2):
                    sp.wait_ge(s["norm"], at.count(1, -1))
                    sp.dma_start(d["xo"][bass.ds(at.count(1, -2), 1)].rearrange("o p c -> (o p) c"), XN[at.c % 2][:, :])\
                        .then_inc(xo_out[at.c % 2], 16)
                if at.plus(1).exists():
                    guard_rows(at.plus(1))

            run(sp, unit, PER, U)
            for u in (U - 2, U - 1):
                sp.wait_ge(s["norm"], u + 1)
                sp.dma_start(d["xo"][u], XN[u % 2][:, :]).then_inc(xo_out[u % 2], 16)
            for p in range(2):
                sp.wait_ge(xo_out[p], 16 * U // 2)

        @block.gpsimd
        def _(pool):
            for p in range(2):
                ins = nc.gpsimd.memset(Q[p][:, :, :], 0.0)
            ins.then_inc(s["init"], 1)

            def unit(at):
                p = at.c % 2
                pool.wait_ge(qd_in[p], at.even(1) * (16 * NQD) + 16 * NQD)
                v = QD[p][:, :, :].rearrange("p h (b j) -> p (h b) j", j=QB)
                nc.gpsimd.tensor_tensor(v, v, bc(k["qmask"][:, :], 1, H * P // QB), ALU.mult).then_inc(s["qd_masked"], 1)

            run(pool, unit, PER, U)

        @block.tensor
        def _(pe):
            def row_scores(at, heads):
                p, i = (at.c // T) % 2, at.c % T
                if at.c % T == 0 and heads[0] == 0:
                    pe.wait_ge(kq_in[p], (at.even(T) + 1) * (16 * NKQ))
                for h in heads:
                    if at.since(1) or h >= 2:
                        pe.wait_ge(s["a_used"], at.count(H, h - 1))
                    nc.tensor.matmul(PA[h % 2][:, :], Q[p][0:GROW, h, i * P:(i + 1) * P], K[p][0:GROW, h, :],
                                     start=True, stop=True).then_inc(s["a_ready"], 1)

            def scores(at, c):
                t, g, i, p = c // NG, c % NG, at.c % T, (at.c // T) % 2
                out = SC[c % 2]
                if at.since(1) or c >= 2:
                    pe.wait_ge(s["p_ready"], at.count(SUB, c - 1))
                if c == 0:
                    pe.wait_ge(s["m_in"], at.count(16, 16))
                rows = DROW if t <= i else ROWS
                for hh in range(HG):
                    h = HG * g + hh
                    lhs = K[p][0:rows, h, t * P:(t + 1) * P]
                    if window(t, i):
                        for half in range(2):
                            q0 = i * P + half * 64
                            ins = nc.tensor.matmul(out[:, half, hh * 64:(hh + 1) * 64], lhs, Q[p][0:rows, h, q0:q0 + 64],
                                                   start=hh == 0, stop=True, skip_group_check=True)
                    else:
                        ins = nc.tensor.matmul(out[:, hh // 4, (hh % 4) * P:(hh % 4 + 1) * P], lhs,
                                               Q[p][0:rows, h, i * P:(i + 1) * P],
                                               start=hh % 4 == 0, stop=True, skip_group_check=True)
                if window(t, i):
                    if c == NG * max(i - 1, 0):
                        pe.wait_ge(s["qd_masked"], at.count(1, 1))
                    blocks = {0: range(P // QB), -1: range(2), 1: range(P // QB - 2, P // QB)}[t - i]
                    for b in blocks:
                        z, z0 = (k["zlo"], ZLO_0) if t <= i else (k["zhi"], ZHI_0)
                        x0 = z0 + (t - i) * P - QB * b
                        o = out[:, b // 4, :].rearrange("p (h q) -> p h q", h=HG)[:, :, (b % 4) * QB:(b % 4 + 1) * QB]
                        ins = nc.tensor.matmul(o, z[:, x0:x0 + P], QD[at.c % 2][:, HG * g:HG * g + HG, b * QB:(b + 1) * QB],
                                               start=False, stop=True, skip_group_check=True)
                ins.then_inc(s["s_ready"], 1)

            def value_products(at, t):
                i, p = at.c % T, (at.c // T) % 2
                v = VG[p][:, 0:VW].rearrange("p (s t h c) -> p s t h c", s=2, t=T, h=H)
                if t == 0 and at.since(1):
                    pe.wait_ge(s["xt_ready"], at.count(1))
                if t == 0 and i == 0:
                    pe.wait_ge(v_in[p], (at.even(T) + 1) * 16)
                pe.wait_ge(s["p_ready"], at.count(SUB, NG * (t + 1)))
                for g in range(H // NQ4):
                    for a in range(NQ4):
                        h = NQ4 * a + g
                        nc.tensor.matmul(PV[32 * a:32 * a + V16, g * P:(g + 1) * P], v[:, 0 if t <= i else 1, t, h, :],
                                         PR[at.c % 2][:, t, h, :], start=(t == 0 and g == 0), stop=True,
                                         skip_group_check=True)

            def relative_values(at, half):
                i = at.c % T
                for n in range(P // (2 * WB)):
                    qb = half * P // (2 * WB) + n
                    jobs = [(i, k["tvd"], P - WB - WB * qb)]
                    if i > 0 and qb < CW // WB:
                        jobs.append((i - 1, k["tvm"], CW - WB - WB * qb))
                    if i < T - 1 and qb >= (P - CW) // WB:
                        jobs.append((i + 1, k["tvp"], P - WB - WB * qb))
                    r0, grp = (n % WR) * WB * HD, n // WR
                    for j, (t, tab, q0) in enumerate(jobs):
                        ins = nc.tensor.matmul(MI[r0:r0 + WB * HD, grp * H * WB:(grp + 1) * H * WB],
                                               tab[:, q0 * HD:(q0 + WB) * HD], PR[at.c % 2][:, t, :, qb * WB:(qb + 1) * WB],
                                               start=j == 0, stop=j == len(jobs) - 1)
                ins.then_inc(s["w_ready"], 1)

            def relative_value_sums(at):
                pe.wait_ge(s["w_masked"], at.count(2, 2))
                for b in range(WR):
                    for a in range(NQ4):
                        o = PV[32 * a:32 * a + V16, :].rearrange("p (h g b q) -> p h g b q", h=NQ4, b=WR, q=WB)[:, :, :, b, :]
                        w = WM[:, :, :, NQ4 * a:NQ4 * a + NQ4, :].rearrange("p c g h q -> p h (c g) q")
                        ins = nc.tensor.matmul(o, k["red"][:, b, :], w, start=False, stop=True, skip_group_check=True)
                ins.then_inc(s["pv_ready"], 1)

            def guard_transpose(at):
                pe.wait_ge(s["mp_ready"], at.count(1, 1))
                nc.tensor.transpose(MIB, NP[:, :, :].rearrange("p c h -> p (c h)"), idb[:, :]).then_inc(s["mt_ready"], 1)

            def output_transposes(at):
                pe.wait_ge(s["xt_ready"], at.count(1, 1))
                for g in range(NQ4):
                    ins = nc.tensor.transpose(MI[:, g * P:(g + 1) * P], XT[:, g * P:(g + 1) * P], k["ident"][:, :])
                ins.then_inc(s["xtt_ready"], 1)

            MIB = MI[0:6 * H, 0:P // 2].bitcast(BF16)
            pe.wait_ge(s["init"], 4)
            row_scores(at0(0), range(H))
            guard_transpose(at0(0))
            row_scores(at0(1), range(H))

            def unit(at):
                before = at.plus(-1)
                for c in range(SUB):
                    if at.plus(2).exists():
                        row_scores(at.plus(2), range(2 * c, 2 * c + 2))
                    scores(at, c)
                    if before.exists():
                        if c == 0:
                            value_products(before, T - 1)
                        if c == 1:
                            if at.since(2):
                                pe.wait_ge(s["norm"], at.count(1, -1))
                            else:
                                pe.wait_ge(s["mt_copied"], 2)
                            relative_values(before, 0)
                        if c == 2:
                            pe.wait_ge(s["w_masked"], before.count(2, 1))
                            relative_values(before, 1)
                        if c == 3:
                            relative_value_sums(before)
                    if c == 3 and at.plus(1).exists():
                        if not at.since(1):
                            pe.wait_ge(s["mt_copied"], 1)
                        guard_transpose(at.plus(1))
                    if c == 4:
                        if before.exists():
                            if at.plus(1).exists():
                                pe.wait_ge(s["mt_copied"], at.count(1, 2))
                            output_transposes(before)
                        value_products(at, 0)
                    if c == 5:
                        value_products(at, 1)
                    if c == 7:
                        value_products(at, 2)

            run(pe, unit, PER, U)
            end = at0(U - 1)
            value_products(end, T - 1)
            pe.wait_ge(s["norm"], U - 1)
            relative_values(end, 0)
            pe.wait_ge(s["w_masked"], 2 * U - 1)
            relative_values(end, 1)
            relative_value_sums(end)
            output_transposes(end)

        @block.scalar
        def _(act):
            def exponentials(at, c):
                t, g, i = c // NG, c % NG, at.c % T
                act.wait_ge(s["s_ready"], at.count(SUB, c + 1))
                if c == 0 and at.since(2):
                    act.wait_ge(s["w_ready"], at.count(2, -2))
                out = PR[at.c % 2][:, t, HG * g:HG * g + HG, :]
                if window(t, i):
                    src = SC[c % 2][:, :, :].rearrange("p c (h q) -> p c h q", h=HG)
                    out = out.rearrange("p h (c q) -> p c h q", c=2)
                else:
                    src = SC[c % 2][:, :, :].rearrange("p c (h q) -> p (c h) q", q=P)
                nc.scalar.activation(out, src, ACT.Exp, scale=SCALE).then_inc(s["p_ready"], 1)

            def guard_copy(at):
                act.wait_ge(s["mt_ready"], at.count(1, 1))
                if at.since(1):
                    act.wait_ge(s["m_out"], at.count(16))
                nc.scalar.copy(MT[:, :], MI[0:6 * H, 0:P // 2].bitcast(BF16)).then_inc(s["mt_copied"], 1)

            def output_copy(at):
                act.wait_ge(s["pv_ready"], at.count(1, 1))
                if at.since(1):
                    act.wait_ge(s["xtt_ready"], at.count(1))
                nc.scalar.copy(XT[:, :], PV[:, :]).then_inc(s["xt_ready"], 1)

            guard_copy(at0(0))

            def unit(at):
                for c in range(SUB):
                    exponentials(at, c)
                    if c == 3 and at.plus(-1).exists():
                        output_copy(at.plus(-1))
                    if c == 3 and at.plus(1).exists():
                        guard_copy(at.plus(1))

            run(act, unit, PER, U)
            output_copy(at0(U - 1))

        @block.vector
        def _(dve):
            for p in range(2):
                nc.vector.memset(K[p][0:GROW, :, :], 0.0)
            for p in range(2):
                nc.vector.memset(K[p][GROW:P, :, :], 1.0).then_inc(s["init"], 1)
            nc.vector.memset(PV[:, :], 0.0)
            nc.vector.tensor_copy(idb[:, :], k["ident"][:, :]).then_inc(s["init"], 1)

            def row_max(at, heads):
                for h in heads:
                    dve.wait_ge(s["a_ready"], at.count(H, h + 1))
                    nc.vector.reduce_max(MX[at.c % 2][:, h:h + 1], PA[h % 2][:, :], AX_X).then_inc(s["a_used"], 1)

            def link(at, n, ins):
                ins.then_inc(s["dv"], 1)
                dve.wait_ge(s["dv"], at.count(MCH - 1, n))

            def guard_parts(at):
                p, i = (at.c // T) % 2, at.c % T
                dve.wait_ge(s["a_used"], at.count(H, H))
                if i == 0:
                    dve.wait_ge(v_in[p], (at.even(T) + 1) * 16)
                if at.since(1):
                    dve.wait_ge(s["mt_ready"], at.count(1))
                g = VG[p][:, VW + i * H:VW + (i + 1) * H]
                nc.vector.tensor_copy(NP[:, 3:6, :], VG[p][:, VW + T * H:VGW].rearrange("p (c t h) -> p c t h", c=3, t=T)[:, :, i, :])
                link(at, 1, nc.vector.scalar_tensor_tensor(out=nm[:, :], in0=MX[at.c % 2][:, :], scalar=-1.0, in1=g,
                                                           op0=ALU.mult, op1=ALU.subtract))
                link(at, 2, nc.vector.tensor_copy(NP[:, 0, :], nm[:, :]))
                link(at, 3, nc.vector.tensor_tensor(r1[:, :], nm[:, :], NP[:, 0, :], ALU.subtract))
                link(at, 4, nc.vector.tensor_copy(NP[:, 1, :], r1[:, :]))
                link(at, 5, nc.vector.tensor_tensor(r2[:, :], r1[:, :], NP[:, 1, :], ALU.subtract))
                nc.vector.tensor_copy(NP[:, 2, :], r2[:, :]).then_inc(s["mp_ready"], 1)

            def keep_values(at, half):
                dve.wait_ge(s["w_ready"], at.count(2, half + 1))
                if at.since(1):
                    dve.wait_ge(s["pv_ready"], at.count(1))
                nc.vector.tensor_tensor(WM[:, half, :, :, :].rearrange("p g h q -> p (g h) q"),
                                        MI[:, :].rearrange("p (n q) -> p n q", q=WB),
                                        bc(k["wmask"][:, :], 1, S // WB), ALU.mult).then_inc(s["w_masked"], 1)

            def normalise(at):
                dve.wait_ge(s["xtt_ready"], at.count(1, 1))
                v = MI[:, :].rearrange("p (n c) -> p n c", c=32)
                nc.vector.reciprocal(RD[:, :], v[:, :, HD]).then_inc(s["rd"], 1)
                dve.wait_ge(s["rd"], at.count(1, 1))
                if at.since(2):
                    dve.wait_ge(xo_out[at.c % 2], at.even(1) * 16)
                xn = XN[at.c % 2][:, :].rearrange("p (a g d) -> p g a d", a=NQ4, d=HD)
                nc.vector.tensor_tensor(xn, MI[:, :].rearrange("p (g a c) -> p g a c", g=NQ4, a=NQ4)[:, :, :, 0:HD],
                                        bc(RD[:, :].rearrange("p (g a) -> p g a", g=NQ4), 3, HD), ALU.mult).then_inc(s["norm"], 1)

            row_max(at0(0), range(H))
            guard_parts(at0(0))
            row_max(at0(1), range(H))

            def unit(at):
                before = at.plus(-1)
                if at.plus(1).exists():
                    guard_parts(at.plus(1))
                for c in range(SUB):
                    if at.plus(2).exists():
                        row_max(at.plus(2), range(2 * c, 2 * c + 2))
                    if at.plus(-1).exists():
                        if c in (1, 2):
                            keep_values(before, c - 1)
                        if c == 4:
                            normalise(before)

            run(dve, unit, PER, U)
            end = at0(U - 1)
            keep_values(end, 0)
            keep_values(end, 1)
            normalise(end)


def stage_output(nc, m, k, d):
    XA, X, X1 = ([m.sb(f"c_{n}{p}", [P, T, E]) for p in range(2)] for n in ("xa", "x", "x1"))
    XNT = [m.sb(f"c_xnT{p}", [P, S]) for p in range(2)]
    xn, fin, aT = m.sb("c_xn", [P, T, E]), m.sb("c_fin", [P, T, E]), m.sb("c_aT", [P, S])
    sg, hh = m.sb("c_sg", [P, FC, S]), m.sb("c_hh", [P, FC, S])
    tmp = {"st": m.sb("c_st", [P, T, 6]), "mv": m.sb("c_mv", [P, T, 2]), "std": m.sb("c_std", [P, T]),
           "rstd": m.sb("c_rstd", [P, T]), "gap": m.sb("c_gap", [P, 1])}
    pT, py, po = m.ps("c_pt", [P, S]), m.ps("c_py", [P, S]), m.ps("c_po", [P, S])
    PG, PU = ([m.ps(f"c_p{n}{p}", [P, S]) for p in range(2)] for n in "gu")
    names = ("in0", "in1", "xb", "aT", "aTs", "y", "x1", "var", "std", "xn", "xT", "xTs", "gate", "up", "silu", "hid",
             "down", "fin", "out", "dv")
    s = {n: m.sem("c_s_" + n) for n in names}
    x_in = [s[f"in{p}"] for p in range(2)]
    NLINK = 2

    def at0(c):
        return At(0, c, 2, B)

    with nc.Block() as block:
        @block.sync
        def _(sp):
            def load(at):
                p = at.c % 2
                sp.dma_start(XA[p][:, :, :], d["xo"][bass.ds(at.count(T), T)].rearrange("t p e -> p t e")).then_inc(x_in[p], 16)
                sp.dma_start(X[p][:, :, :], d["x"][bass.ds(at.count(), 1)].rearrange("o (t p) e -> p (o t) e", p=P)).then_inc(x_in[p], 16)

            load(at0(0))
            load(at0(1))

            def step(at):
                if at.plus(2).exists():
                    sp.wait_ge(s["x1"], at.count(1, 1))
                    load(at.plus(2))
                sp.wait_ge(s["fin"], at.count(1, 1))
                sp.dma_start(d["out"][bass.ds(at.count(), 1)].rearrange("o (t p) e -> p (o t) e", p=P), fin[:, :, :]).then_inc(s["out"], 16)

            run(sp, step, 2, B)
            sp.wait_ge(s["out"], 16 * B)

        @block.gpsimd
        def _(pool):
            def step(at):
                x = X[at.c % 2]
                pool.wait_ge(x_in[at.c % 2], at.even(1) * 32 + 32)
                nc.gpsimd.tensor_tensor(x[:, :, :], x[:, :, :], bc(k["bo"][:, :], 1, T), ALU.add).then_inc(s["xb"], 1)

            run(pool, step, 2, B)

        @block.tensor
        def _(pe):
            def output_projection(at):
                pe.wait_ge(x_in[at.c % 2], at.even(1) * 32 + 32)
                if at.since(1):
                    pe.wait_ge(s["xTs"], at.count())
                for t in range(T):
                    ins = nc.tensor.transpose(pT[:, t * P:(t + 1) * P], XA[at.c % 2][:, t, :], k["ident"][:, :])
                ins.then_inc(s["aT"], 1)
                pe.wait_ge(s["aTs"], at.count(1, 1))
                if at.since(1):
                    pe.wait_ge(s["x1"], at.count())
                for t in range(T):
                    ins = nc.tensor.matmul(py[:, t * P:(t + 1) * P], aT[:, t * P:(t + 1) * P], k["wo"][:, :], start=True, stop=True)
                ins.then_inc(s["y"], 1)

            def row_transposes(at):
                pe.wait_ge(s["xn"], at.count(1, 1))
                for t in range(T):
                    ins = nc.tensor.transpose(pT[:, t * P:(t + 1) * P], xn[:, t, :], k["ident"][:, :])
                ins.then_inc(s["xT"], 1)

            def gate_and_up(at):
                pe.wait_ge(s["xTs"], at.count(1, 1))
                for c in range(FC):
                    n = (at.c * FC + c) % 2
                    if c >= 2 or at.since(1):
                        pe.wait_ge(s["hid"], at.count(FC, c - 1))
                    nc.tensor.matmul(PG[n][:, :], k["wg"][:, c * P:(c + 1) * P], XNT[at.c % 2][:, :], start=True, stop=True).then_inc(s["gate"], 1)
                    nc.tensor.matmul(PU[n][:, :], k["wu"][:, c * P:(c + 1) * P], XNT[at.c % 2][:, :], start=True, stop=True).then_inc(s["up"], 1)

            def down(at):
                pe.wait_ge(s["hid"], at.count(FC, FC))
                if at.since(1):
                    pe.wait_ge(s["fin"], at.count())
                for t in range(T):
                    for c in range(FC):
                        ins = nc.tensor.matmul(po[:, t * P:(t + 1) * P], hh[:, c, t * P:(t + 1) * P], k["wd"][:, c, :],
                                               start=c == 0, stop=c == FC - 1)
                ins.then_inc(s["down"], 1)

            output_projection(at0(0))
            row_transposes(at0(0))

            def step(at):
                after = at.plus(1)
                if after.exists():
                    output_projection(after)
                gate_and_up(at)
                if after.exists():
                    row_transposes(after)
                down(at)

            run(pe, step, 2, B)

        @block.scalar
        def _(act):
            def transposed_attention(at):
                act.wait_ge(s["aT"], at.count(1, 1))
                nc.scalar.copy(aT[:, :], pT[:, :]).then_inc(s["aTs"], 1)

            def root(at):
                act.wait_ge(s["var"], at.count(1, 1))
                nc.scalar.activation(tmp["std"][:, :], tmp["mv"][:, :, 1], ACT.Sqrt, bias=k["eps"][:, 0:1]).then_inc(s["std"], 1)

            def transposed_rows(at):
                act.wait_ge(s["xT"], at.count(1, 1))
                nc.scalar.copy(XNT[at.c % 2][:, :], pT[:, :]).then_inc(s["xTs"], 1)

            transposed_attention(at0(0))
            root(at0(0))
            transposed_rows(at0(0))

            def step(at):
                after = at.plus(1)
                if after.exists():
                    transposed_attention(after)
                    root(after)
                for c in range(FC):
                    act.wait_ge(s["gate"], at.count(FC, c + 1))
                    if at.since(1):
                        act.wait_ge(s["hid"], at.count(FC, c - FC + 1))
                    nc.scalar.activation(sg[:, c, :], PG[(at.c * FC + c) % 2][:, :], ACT.Silu).then_inc(s["silu"], 1)
                if after.exists():
                    transposed_rows(after)

            run(act, step, 2, B)

        @block.vector
        def _(dve):
            def linker(at, done):
                def link(ins):
                    nonlocal done
                    done += 1
                    ins.then_inc(s["dv"], 1)
                    dve.wait_ge(s["dv"], at.count(NLINK, done))
                return link

            def residual(at):
                p = at.c % 2
                if at.since(2):
                    dve.wait_ge(s["fin"], at.count(1, -1))
                dve.wait_ge(s["y"], at.count(1, 1))
                dve.wait_ge(s["xb"], at.count(1, 1))
                nc.vector.tensor_tensor(X1[p][:, :, :], py[:, :].rearrange("p (t e) -> p t e", t=T), X[p][:, :, :], ALU.add).then_inc(s["x1"], 1)
                dve.wait_ge(s["x1"], at.count(1, 1))
                layernorm_statistics(nc, X1[p], tmp, linker(at, 0), s["var"])

            def normalise(at):
                dve.wait_ge(s["std"], at.count(1, 1))
                if at.since(1):
                    dve.wait_ge(s["xT"], at.count())
                layernorm_rows(nc, X1[at.c % 2], xn, tmp, linker(at, 1)).then_inc(s["xn"], 1)

            def hidden(at, c):
                dve.wait_ge(s["silu"], at.count(FC, c + 1))
                dve.wait_ge(s["up"], at.count(FC, c + 1))
                if at.since(1):
                    dve.wait_ge(s["down"], at.count())
                nc.vector.tensor_tensor(hh[:, c, :], sg[:, c, :], PU[(at.c * FC + c) % 2][:, :], ALU.mult).then_inc(s["hid"], 1)

            residual(at0(0))
            normalise(at0(0))

            def step(at):
                after = at.plus(1)
                if after.exists():
                    residual(after)
                    normalise(after)
                for c in range(FC):
                    hidden(at, c)
                dve.wait_ge(s["down"], at.count(1, 1))
                if at.since(1):
                    dve.wait_ge(s["out"], at.count(16))
                nc.vector.tensor_tensor(fin[:, :, :], po[:, :].rearrange("p (t e) -> p t e", t=T), X1[at.c % 2][:, :, :], ALU.add).then_inc(s["fin"], 1)

            run(dve, step, 2, B)


def program(nc, d):
    for name, shape, dt in (("qop", (B, SLOTS, P, S), BF16), ("kop", (B, SLOTS, P, S), BF16),
                            ("qf", (B, P, S), F32), ("vg", (B, P, VGW), F32), ("xo", (U, P, E), F32),
                            ("gt", (2, 6 * H, P), BF16)):
        d[name] = nc.dram_tensor("scratch_" + name, shape, dt, kind="Internal").ap()
    with ExitStack() as keep:
        m = Memory(nc, keep)
        k = {"ident": m.sb("ident", [P, P]), "qmask": m.sb("qmask", [P, QB]), "wmask": m.sb("wmask", [P, WB]),
             "red": m.sb("red", [P, WR, V16]), "zlo": m.sb("zlo", [P, ZLO_W]), "zhi": m.sb("zhi", [P, ZHI_W]),
             "tvd": m.sb("tvd", [P, P * HD]), "tvm": m.sb("tvm", [P, CW * HD]), "tvp": m.sb("tvp", [P, CW * HD]),
             "wq": m.sb("wq", [P, P]), "wk": m.sb("wk", [P, P]), "wv": m.sb("wv", [P, P]), "wo": m.sb("wo", [P, P]),
             "bq": m.sb("bq", [P, 1]), "bk0": m.sb("bk0", [P, 1]), "relend": m.sb("relend", [P, H]),
             "bv2": m.sb("bv2", [P, 2, P]), "bo": m.sb("bo", [P, P]), "relbd": m.sb("relbd", [P, 2, H * REL], BF16),
             "wg": m.sb("wg", [P, F]), "wu": m.sb("wu", [P, F]), "wd": m.sb("wd", [P, FC, P]), "eps": m.sb("eps", [P, 1])}
        for stage in (setup_constants, stage_project, stage_attend, stage_output):
            with ExitStack() as ctx:
                stage(nc, Memory(nc, ctx), k, d)


def kernel(**inputs):
    import concourse.bacc as _bacc
    from concourse.bass_utils import run_bass_kernel_spmd as _run

    a = {n.removeprefix("L0_"): np.asarray(v) for n, v in inputs.items()}
    rel_k, rel_v = a["attn_rel_k"], a["attn_rel_v"]

    def by_d(w):
        return w.reshape(H, HD, *w.shape[1:]).swapaxes(0, 1).reshape(P, *w.shape[1:])

    clipped = np.clip(np.arange(-EXT_0, EXT_0 + 1), -REL, REL) + REL
    arrays = {
        "x": a["attn_hidden_states"],
        "wq": by_d(a["attn_Wq"]).T, "wk": by_d(a["attn_Wk"]).T, "wv": a["attn_Wv"].T, "wo": a["attn_Wo"].T,
        "bq": by_d(a["attn_bq"])[:, None], "bk": by_d(a["attn_bk"])[:, None],
        "bv": a["attn_bv"][None, :], "bo": a["attn_bo"][None, :],
        "rkh": np.repeat(rel_k.T, H, axis=0),
        "rkj": np.tile(rel_k[[0, NREL - 1]].T, (QB, 1)),
        "rkx": rel_k[clipped].T, "rvx": rel_v[clipped], "rv": rel_v,
        "wg": a["ffn_w_gate"].T, "wu": a["ffn_w_up"].T, "wd": a["ffn_w_down"].T,
    }
    arrays = {"in_" + n: np.ascontiguousarray(v) for n, v in arrays.items()}
    nc = _bacc.Bacc("TRN2", target_bir_lowering=False, num_devices=1)
    d = {n[3:]: nc.dram_tensor(n, v.shape, mybir.dt.from_np(v.dtype), kind="ExternalInput").ap() for n, v in arrays.items()}
    d["out"] = nc.dram_tensor("out", (B, S, E), F32, kind="ExternalOutput").ap()
    program(nc, d)
    r = _run(nc, [arrays], core_ids=[0])
    return r.results[0]["out"]
```

```python
from contextlib import ExitStack

import numpy as np

import concourse.bass as bass
from concourse import mybir

F32 = mybir.dt.float32
BF16 = mybir.dt.bfloat16
I32 = mybir.dt.int32
ALU = mybir.AluOpType
ACT = mybir.ActivationFunctionType
AX_X, AX_XY = mybir.AxisListType.X, mybir.AxisListType.XY

ONES_BF16 = float(np.array([0x3F803F80], np.uint32).view(np.float32)[0])

P = 128
B, S, E = 16, 512, 128
H, HD = 16, 8
REL = 20
NREL = 2 * REL + 1
T = S // P
U = B * T
F = 384
FC = F // P
EPS = 1e-5

SLOTS = 6
K_SLOT = {0: (0, 3, 5), 1: (1, 4), 2: (2,)}
Q_SLOT = {0: (0, 1, 2), 1: (3, 4), 2: (5,)}
PARTS = 3
OPR = SLOTS * HD
GROW = 96
DROW = GROW + 3
ROWS = DROW + 3

HG = 8
NG = H // HG
SUB = T * NG
QB = 2
QROW = 64
QROWS = QROW * (QB - 1) + OPR
WB = 8
WR = P // (WB * HD)
CW = -(-REL // WB) * WB
V16 = 16
NQ4 = 4

ZLO_0 = P + REL - QB
ZLO_W = ZLO_0 + P
ZHI_0 = -QB
ZHI_W = ZHI_0 + REL + P
EXT_0 = 176
EXT = 2 * EXT_0 + 1
VW = 2 * T * H * V16
VGW = VW + 4 * T * H


def bc(ap, axis, n):
    ap = ap.unsqueeze(axis)
    shape = list(ap.shape)
    shape[axis] = n
    return ap.to_broadcast(shape)


class At:

    def __init__(self, it, c, per, total):
        self.it, self.c, self.per, self.total = it, c, per, total
        self.fixed = isinstance(it, int)

    def plus(self, n):
        return At(self.it, self.c + n, self.per, self.total)

    def count(self, each=1, extra=0):
        return self.it * (self.per * each) + (self.c * each + extra)

    def even(self, n):
        return self.it * (self.per // (2 * n)) + self.c // (2 * n)

    def exists(self):
        return not self.fixed or 0 <= self.it * self.per + self.c < self.total

    def since(self, n):
        return not self.fixed or self.it * self.per + self.c >= n


def run(eng, step, per, total):
    for c in range(per):
        step(At(0, c, per, total))
    with eng.Fori(1, total // per - 1) as it:
        for c in range(per):
            step(At(it, c, per, total))
    for c in range(per):
        step(At(total // per - 1, c, per, total))


class Memory:

    def __init__(self, nc, ctx):
        self.nc, self.ctx = nc, ctx

    def sb(self, name, shape, dt=F32):
        return self.ctx.enter_context(self.nc.sbuf_tensor(name, shape, dt))

    def ps(self, name, shape, dt=F32):
        return self.ctx.enter_context(self.nc.psum_tensor(name, shape, dt))

    def sem(self, name):
        return self.ctx.enter_context(self.nc.semaphore(name))


def setup_constants(nc, m, k, d):
    s_ld, s_id, s_z, s_vg, s_v = (m.sem("su_" + n) for n in ("loaded", "pool", "zero", "values", "vector"))
    ones = m.sb("su_ones", [P, P])
    wgi = m.sb("su_wgi", [P, F], I32)
    wui = m.sb("su_wui", [P, F], I32)
    wdi = m.sb("su_wdi", [P, FC, P], I32)
    bkc = m.sb("su_bk", [P, 1])
    rkc, rkj = m.sb("su_rkc", [P, NREL]), m.sb("su_rkj", [P, 2])
    z, slot = m.sb("su_z", [P, ZLO_W + ZHI_W]), m.sb("su_slot", [P, PARTS])
    zp = m.sb("su_zp", [P, ZLO_W + ZHI_W], BF16)
    bvb, rvb = m.sb("su_bvb", [P, P]), m.sb("su_rvb", [P, 2, HD])
    rkd = m.sb("su_rkd", [P, NREL])
    hm = m.sb("su_hm", [P, H])
    loads = []

    def toeplitz_k(dst, width, origin):
        for j in range(QB):
            src = bass.AP(d["rkx"].tensor, EXT_0 - origin - j, [[0, SLOTS], [EXT, HD], [1, width]])
            loads.append((dst[QROW * j:QROW * j + OPR, :], src))

    def toeplitz_v(dst, nq, first):
        src = bass.AP(d["rvx"].tensor, (EXT_0 + first) * HD, [[HD, P], [1, nq * HD]])
        loads.append((dst, src))

    toeplitz_k(z[:, 0:ZLO_W], ZLO_W, ZLO_0)
    toeplitz_k(z[:, ZLO_W:], ZHI_W, ZHI_0)
    for j in range(QB):
        loads += [(rkj[QROW * j:QROW * j + OPR, :], d["rkj"]), (slot[QROW * j:QROW * j + OPR, :], d["slot"])]
    toeplitz_v(k["tvd"][:, :], P, 1 - P)
    toeplitz_v(k["tvm"][:, :], CW, 1 - P - CW)
    toeplitz_v(k["tvp"][:, :], CW, 1)
    for n in ("wq", "wk", "wv", "wo"):
        loads.append((k[n][:, :], d[n]))
    loads += [(wgi[:, :], d["wg"]), (wui[:, :], d["wu"]), (wdi[:, :, :], d["wd"].rearrange("(c p) e -> p c e", p=P)),
              (k["bq"][:, :], d["bq"]), (bkc[:, :], d["bk"]), (rkc[:, :], d["rkh"]),
              (bvb[:, :], d["bv"].to_broadcast([P, P])), (k["bo"][:, :], d["bo"].to_broadcast([P, P])),
              (rvb[:, 0, :], d["rv"][0:1, :].to_broadcast([P, HD])),
              (rvb[:, 1, :], d["rv"][NREL - 1:NREL, :].to_broadcast([P, HD]))]
    with nc.Block() as block:
        @block.sync
        def _(sp):
            sp.wait_ge(s_z, 1)
            for dst, src in loads:
                sp.dma_start(dst, src).then_inc(s_ld, 16)

        @block.gpsimd
        def _(pool):
            n = 0

            def link(ins):
                nonlocal n
                n += 1
                ins.then_inc(s_id, 1)
                pool.wait_ge(s_id, n)

            link(nc.gpsimd.memset(ones[:, :], 1.0))
            link(nc.gpsimd.memset(k["ident"][:, :], 0.0))
            link(nc.gpsimd.affine_select(out=k["ident"][:, :], in_=k["ident"][:, :], compare_op=ALU.not_equal, fill=1.0,
                                         base=0, pattern=[[-1, P]], channel_multiplier=1))
            for b in range(WR):
                w = k["wmask"][b * WB * HD:(b + 1) * WB * HD, :]
                link(nc.gpsimd.affine_select(out=w, in_=ones[b * WB * HD:(b + 1) * WB * HD, 0:WB], compare_op=ALU.is_ge, fill=0.0,
                                             base=-HD * (WB - 1), pattern=[[HD, WB]], channel_multiplier=1))
                link(nc.gpsimd.affine_select(out=w, in_=w, compare_op=ALU.is_ge, fill=0.0,
                                             base=HD * WB - 1, pattern=[[-HD, WB]], channel_multiplier=-1))
            link(nc.gpsimd.memset(k["red"][:, :, :], 0.0))
            for p in range(2):
                nc.gpsimd.memset(k["q"][p][:, :, :].rearrange("p h t -> p (h t)").bitcast(F32), 0.0)
                nc.gpsimd.memset(k["qd"][p][:, :, :].rearrange("p h t -> p (h t)").bitcast(F32), 0.0)
                nc.gpsimd.memset(k["vg"][p][:, 0:VW], 0.0).then_inc(s_vg, 1)

        @block.scalar
        def _(act):
            act.wait_ge(s_id, 1)
            for lo, hi, value in ((0, GROW, 0.0), (GROW, P, 1.0)):
                nc.scalar.activation(k["k"][1][lo:hi, :, :].rearrange("p h t -> p (h t)"),
                                     ones[lo:hi, 0:1].to_broadcast([hi - lo, H * S]), ACT.Copy, scale=value)
            act.wait_ge(s_ld, 16 * len(loads))
            for dst, src in ((k["wg"][:, :], wgi[:, :]), (k["wu"][:, :], wui[:, :]), (k["wd"][:, :, :], wdi[:, :, :])):
                nc.scalar.activation(dst, src, ACT.Copy, scale=float(np.float32(1.0 / 127.0)))

        @block.vector
        def _(dve):
            n = 0

            def link(ins):
                nonlocal n
                n += 1
                ins.then_inc(s_v, 1)
                dve.wait_ge(s_v, n)

            for tile in (z, rkj, slot):
                ins = nc.vector.memset(tile[:, :], 0.0)
            ins.then_inc(s_z, 1)
            nc.vector.memset(k["k"][0][0:GROW, :, :], 0.0)
            nc.vector.memset(k["k"][0][GROW:P, :, :].rearrange("p h t -> p (h t)").bitcast(F32), ONES_BF16)
            dve.wait_ge(s_ld, 16 * len(loads))
            dve.wait_ge(s_id, 3 + 2 * WR + 1)
            link(nc.vector.tensor_scalar(z[:, 0:ZLO_W], z[:, 0:ZLO_W], rkj[:, 0:1], None, ALU.subtract))
            link(nc.vector.tensor_scalar(z[:, ZLO_W:], z[:, ZLO_W:], rkj[:, 1:2], None, ALU.subtract))
            for part in range(PARTS):
                link(nc.vector.tensor_copy(zp[:, :], z[:, :]))
                if part == 0:
                    link(nc.vector.tensor_scalar(k["z"][:, :], zp[:, :], slot[:, 0:1], None, ALU.mult))
                else:
                    link(nc.vector.scalar_tensor_tensor(out=k["z"][:, :], in0=zp[:, :], scalar=slot[:, part:part + 1],
                                                        in1=k["z"][:, :], op0=ALU.mult, op1=ALU.add))
                if part < PARTS - 1:
                    link(nc.vector.tensor_tensor(z[:, :], z[:, :], zp[:, :], ALU.subtract))
            for name, nq, side in (("tvd", P, 0), ("tvm", CW, 0), ("tvp", CW, 1)):
                v = k[name][:, :].rearrange("p (q d) -> p q d", d=HD)
                link(nc.vector.tensor_tensor(v, v, bc(rvb[:, side, :], 1, nq), ALU.subtract))
            link(nc.vector.tensor_tensor(k["bk0"][:, :], bkc[:, :], rkc[:, 0:1], ALU.add))
            for side in range(2):
                link(nc.vector.tensor_tensor(k["bv2"][:, side, :].rearrange("p (h d) -> p h d", d=HD),
                                             bvb[:, :].rearrange("p (h d) -> p h d", d=HD),
                                             bc(rvb[:, side, :], 1, H), ALU.add))
            link(nc.vector.tensor_reduce(hm[:, :], k["ident"][:, :].rearrange("p (d h) -> p h d", h=H), AX_X, ALU.add))
            link(nc.vector.tensor_scalar(rkd[:, :], rkc[:, :], rkc[:, 0:1], None, ALU.subtract))
            link(nc.vector.tensor_scalar(k["relend"][:, :], hm[:, :], rkd[:, NREL - 1:NREL], None, ALU.mult))
            for i in range(2):
                link(nc.vector.tensor_tensor(k["relbd"][:, i, :].rearrange("p (h r) -> p h r", h=H),
                                             bc(rkd[:, 1 + REL * i:1 + REL * (i + 1)], 1, H),
                                             bc(hm[:, :], 2, REL), ALU.mult))
            link(nc.vector.tensor_reduce(k["red"][:, :, 0:HD],
                                         k["ident"][:, :].rearrange("p (b j d) -> p b d j", b=WR, d=HD), AX_X, ALU.add))
            link(nc.vector.tensor_scalar(k["minus"][:, :], k["ident"][:, :], -1.0, None, ALU.mult))
            dve.wait_ge(s_vg, 2)
            for p in range(2):
                nc.vector.memset(k["vg"][p][:, 0:VW].rearrange("p (n c) -> p n c", c=V16)[:, :, HD:HD + 1], 1.0)
            link(nc.vector.memset(k["eps"][:, :], EPS))
            link(nc.vector.memset(k["root"][:, :], -0.5))
            link(nc.vector.memset(k["one"][:, :], 1.0))


def layernorm_statistics(nc, x, tmp, link, s_var):
    for t in range(T):
        ins = nc.vector.bn_stats(tmp["st"][:, t, :], x[:, t, :])
    link(ins)
    nc.vector.memset(tmp["gap"][:, :], 0.0)
    for t in range(T):
        ins = nc.vector.bn_aggr(tmp["mv"][:, t, :], tmp["st"][:, t, :])
    ins.then_inc(s_var, 1)


def inverse_deviation(nc, pool, k, tmp, at, s_var, s_eps, s_rstd):
    pool.wait_ge(s_var, at.count(1, 1))
    nc.gpsimd.tensor_tensor(tmp["std"][:, :], tmp["mv"][:, :, 1], k["eps"][:, 0:1].to_broadcast([P, T]), ALU.add).then_inc(s_eps, 1)
    pool.wait_ge(s_eps, at.count(1, 1))
    nc.gpsimd.tensor_tensor(tmp["rstd"][:, :], tmp["std"][:, :], k["root"][:, 0:1].to_broadcast([P, T]), ALU.pow).then_inc(s_rstd, 1)


def layernorm_rows(nc, x, xn, tmp):
    for t in range(T):
        ins = nc.vector.tensor_scalar(xn[:, t, :], x[:, t, :], tmp["mv"][:, t, 0:1], tmp["rstd"][:, t:t + 1],
                                      ALU.subtract, ALU.mult)
    return ins


def load_score_operands(sp, k, d, batch, p):
    for name, dst, slots_of in (("kop", k["k"][p], K_SLOT), ("qop", k["q"][p], Q_SLOT)):
        for part, slots in slots_of.items():
            src = d[name][bass.ds(batch, 1), part].rearrange("o (d h) t -> (o d) h t", h=H)
            if name == "qop":
                sp.dma_start(dst[slots[0] * HD:(slots[-1] + 1) * HD, :, :], bc(src, 0, len(slots))).then_inc(k["kq_in"][p], 16)
            else:
                for n in slots:
                    sp.dma_start(dst[n * HD:(n + 1) * HD, :, :], src).then_inc(k["kq_in"][p], 16)


def stage_project(nc, m, k, d):
    X = [m.sb(f"a_x{p}", [P, T, E]) for p in range(2)]
    xn = m.sb("a_xn", [P, T, E])
    xnT = m.sb("a_xnT", [P, S])
    QF = [m.sb(f"a_qf{p}", [P, S]) for p in range(2)]
    PB = [m.sb(f"a_parts{p}", [P, 2, PARTS, S], BF16) for p in range(2)]
    VT = k["vg"]
    VR = [m.sb(f"a_vr{p}", [P, S]) for p in range(2)]
    qr = m.sb("a_qr", [P, S])
    db, dr = m.sb("a_db", [P, 3, T * H], BF16), m.sb("a_dr", [P, T * H])
    gr = m.sb("a_gr", [P, T, H])
    tmp = {"st": m.sb("a_st", [P, T, 6]), "mv": m.sb("a_mv", [P, T, 2]), "std": m.sb("a_std", [P, T]),
           "rstd": m.sb("a_rstd", [P, T]), "gap": m.sb("a_gap", [P, 1])}
    pT, pq, pk, pv = (m.ps(f"a_p{n}", [P, S]) for n in "tqkv")
    pd = pq[:, 0:T * H]
    PR = [m.ps(f"a_pr{p}", [P, 2, S]) for p in range(2)]
    names = ("x_in0", "x_in1", "var", "eps", "rstd", "xn", "xT", "xTs", "proj", "qevac", "kevac",
             "kless", "kpart", "qsplit", "ksplit", "vevac", "ends", "dsplit", "rel", "relmax", "vdone", "out0", "out1", "dv", "stats", "pl")
    s = {n: m.sem("a_s_" + n) for n in names}
    x_in, out = ([s[f"{n}{p}"] for p in range(2)] for n in ("x_in", "out"))
    NLINK = 3
    NOUT = 2 + 2

    def at0(c):
        return At(0, c, 2, B)

    with nc.Block() as block:
        @block.sync
        def _(sp):
            def load_x(at):
                sp.dma_start(X[at.c % 2][:, :, :],
                             d["x"][bass.ds(at.count(), 1)].rearrange("o (t p) e -> p (o t) e", p=P)).then_inc(x_in[at.c % 2], 16)

            load_x(at0(0))
            load_x(at0(1))

            def step(at):
                p = at.c % 2
                if at.plus(2).exists():
                    sp.wait_ge(s["xn"], at.count(1, 1))
                    load_x(at.plus(2))
                if not at.plus(1).exists():
                    sp.wait_ge(out[0], 16 * NOUT * (B // 2 - 1))
                    load_score_operands(sp, k, d, 0, 0)
                v, guard = (d[n][bass.ds(at.count(), 1)].rearrange("o p t -> p (o t)") for n in ("v", "guard"))
                dsts = [d[n][bass.ds(at.count(), 1)].rearrange("o s p t -> p (o s) t") for n in ("qop", "kop")]
                for n, ready in ((0, "qsplit"), (1, "ksplit")):
                    sp.wait_ge(s[ready], at.count(1, 1))
                    sp.dma_start(dsts[n], PB[p][:, n, :, :]).then_inc(out[p], 16)
                sp.wait_ge(s["vevac"], at.count(1, 1))
                sp.dma_start(v, VR[p][:, :]).then_inc(out[p], 16)
                sp.wait_ge(s["vdone"], at.count(1, 1))
                sp.dma_start(guard, VT[p][:, VW:]).then_inc(out[p], 16)

            run(sp, step, 2, B)
            for p in range(2):
                sp.wait_ge(out[p], 16 * NOUT * B // 2)

        @block.tensor
        def _(pe):
            def transposes(at):
                pe.wait_ge(s["xn"], at.count(1, 1))
                if at.since(1):
                    pe.wait_ge(s["xTs"], at.count())
                for t in range(T):
                    ins = nc.tensor.transpose(pT[:, t * P:(t + 1) * P], xn[:, t, :], k["ident"][:, :])
                ins.then_inc(s["xT"], 1)

            def project(at, n):
                if n == 0:
                    pe.wait_ge(s["xTs"], at.count(1, 1))
                    if at.since(1):
                        pe.wait_ge(s["dsplit"], at.count())
                if n == 1 and at.since(1):
                    pe.wait_ge(s["ksplit"], at.count())
                if n < 2:
                    nc.tensor.matmul((pq, pk)[n][:, :], k[("wq", "wk")[n]][:, :], xnT[:, :],
                                     start=True, stop=True).then_inc(s["proj"], 1)
                    return
                if at.since(1):
                    pe.wait_ge(s["vevac"], at.count())
                for t in range(T):
                    ins = nc.tensor.matmul(pv[:, t * P:(t + 1) * P], xnT[:, t * P:(t + 1) * P], k["wv"][:, :],
                                           start=True, stop=True)
                ins.then_inc(s["proj"], 1)

            def ends(at):
                pe.wait_ge(s["qevac"], at.count(1, 1))
                for t in range(T):
                    ins = nc.tensor.matmul(pd[:, t * H:(t + 1) * H], QF[at.c % 2][:, t * P:(t + 1) * P],
                                           k["relend"][:, :], start=True, stop=True)
                ins.then_inc(s["ends"], 1)

            def relative_terms(at, t):
                if t >= 2 or at.since(1):
                    pe.wait_ge(s["relmax"], at.count(T, t - 1))
                for i in range(2):
                    ins = nc.tensor.matmul(PR[t % 2][:, i, 0:H * REL], PB[at.c % 2][:, 0, 0, t * P:(t + 1) * P],
                                           k["relbd"][:, i, :], start=True, stop=True)
                ins.then_inc(s["rel"], 1)

            def subtract_k_part(at, part):
                pe.wait_ge(s[("kevac", "kpart")[part]], at.count(1, 1))
                nc.tensor.matmul(pk[:, :], k["minus"][:, :], PB[at.c % 2][:, 1, part, :],
                                 start=False, stop=True, skip_group_check=True).then_inc(s["kless"], 1)

            transposes(at0(0))
            for n in range(3):
                project(at0(0), n)
            subtract_k_part(at0(0), 0)

            def step(at):
                after = at.plus(1)
                ends(at)
                relative_terms(at, 0)
                if after.exists():
                    transposes(after)
                subtract_k_part(at, 1)
                relative_terms(at, 1)
                if after.exists():
                    project(after, 0)
                relative_terms(at, 2)
                if after.exists():
                    project(after, 1)
                relative_terms(at, 3)
                if after.exists():
                    project(after, 2)
                if after.exists():
                    subtract_k_part(after, 0)

            run(pe, step, 2, B)

        @block.scalar
        def _(act):
            def rows(at):
                act.wait_ge(s["xT"], at.count(1, 1))
                if at.since(1):
                    act.wait_ge(s["proj"], at.count(3))
                nc.scalar.copy(xnT[:, :], pT[:, :]).then_inc(s["xTs"], 1)

            def part(at, n, part, bank):
                bias = k[("bq", "bk0")[n]][:, 0:1]
                return nc.scalar.activation(PB[at.c % 2][:, n, part, :], bank[:, :], ACT.Identity, bias=bias)

            def projected(at):
                act.wait_ge(s["proj"], at.count(3, 1))
                if at.since(2):
                    act.wait_ge(out[at.c % 2], at.even(1) * (16 * NOUT))
                part(at, 0, 0, pq)
                nc.scalar.activation(QF[at.c % 2][:, :], pq[:, :], ACT.Identity, bias=k["bq"][:, 0:1]).then_inc(s["qevac"], 1)
                act.wait_ge(s["proj"], at.count(3, 2))
                part(at, 1, 0, pk).then_inc(s["kevac"], 1)
                act.wait_ge(s["proj"], at.count(3, 3))
                nc.scalar.copy(VR[at.c % 2][:, :], pv[:, :]).then_inc(s["vevac"], 1)
                act.wait_ge(s["kless"], at.count(2, 1))
                part(at, 1, 1, pk).then_inc(s["kpart"], 1)

            rows(at0(0))
            projected(at0(0))

            def step(at):
                if at.plus(1).exists():
                    rows(at.plus(1))
                act.wait_ge(s["kless"], at.count(2, 2))
                part(at, 1, 2, pk).then_inc(s["ksplit"], 1)
                if at.plus(1).exists():
                    projected(at.plus(1))

            run(act, step, 2, B)

        @block.gpsimd
        def _(pool):
            def deviation(at):
                inverse_deviation(nc, pool, k, tmp, at, s["var"], s["eps"], s["rstd"])

            deviation(at0(0))
            deviation(at0(1))

            def step(at):
                p = at.c % 2
                pool.wait_ge(s["qevac"], at.count(1, 1))
                if at.since(1):
                    pool.wait_ge(s["qsplit"], at.count())
                nc.gpsimd.tensor_tensor(qr[:, :], QF[p][:, :], PB[p][:, 0, 0, :], ALU.subtract)
                nc.gpsimd.tensor_tensor(PB[p][:, 0, 1, :], QF[p][:, :], PB[p][:, 0, 0, :], ALU.subtract).then_inc(s["pl"], 1)
                pool.wait_ge(s["pl"], at.count(1, 1))
                nc.gpsimd.tensor_tensor(PB[p][:, 0, 2, :], qr[:, :], PB[p][:, 0, 1, :], ALU.subtract).then_inc(s["qsplit"], 1)
                if at.plus(2).exists():
                    deviation(at.plus(2))

            run(pool, step, 2, B)

        @block.vector
        def _(dve):
            def linker(at, done):
                def link(ins):
                    nonlocal done
                    done += 1
                    ins.then_inc(s["dv"], 1)
                    dve.wait_ge(s["dv"], at.count(NLINK, done))
                return link

            def statistics(at):
                p = at.c % 2

                def link(ins):
                    ins.then_inc(s["stats"], 1)
                    dve.wait_ge(s["stats"], at.count(1, 1))

                dve.wait_ge(x_in[p], at.even(1) * 16 + 16)
                layernorm_statistics(nc, X[p], tmp, link, s["var"])

            def normalise(at):
                dve.wait_ge(s["rstd"], at.count(1, 1))
                if at.since(1):
                    dve.wait_ge(s["xT"], at.count())
                layernorm_rows(nc, X[at.c % 2], xn, tmp).then_inc(s["xn"], 1)

            for b in range(2):
                statistics(at0(b))
                normalise(at0(b))

            def step(at):
                p = at.c % 2
                link = linker(at, 0)

                def maxima(t):
                    dve.wait_ge(s["rel"], at.count(T, t + 1))
                    nc.vector.tensor_reduce(gr[:, t, :], PR[t % 2][:, :, 0:H * REL].rearrange("p c (h r) -> p h c r", h=H), AX_XY,
                                            ALU.max).then_inc(s["relmax"], 1)

                dve.wait_ge(s["ends"], at.count(1, 1))
                link(nc.vector.tensor_copy(db[:, 0, :], pd[:, :]))
                nc.vector.tensor_tensor(dr[:, :], pd[:, :], db[:, 0, :], ALU.subtract).then_inc(s["dsplit"], 1)
                maxima(0)
                dve.wait_ge(s["dsplit"], at.count(1, 1))
                link(nc.vector.tensor_copy(db[:, 1, :], dr[:, :]))
                link(nc.vector.tensor_tensor(db[:, 2, :], dr[:, :], db[:, 1, :], ALU.subtract))
                nc.vector.tensor_copy(VT[p][:, VW + T * H:VGW], db[:, :, :].rearrange("p c n -> p (c n)"))
                maxima(1)
                if at.plus(2).exists():
                    statistics(at.plus(2))
                maxima(2)
                maxima(3)
                dve.wait_ge(s["relmax"], at.count(T, T))
                nc.vector.tensor_scalar(VT[p][:, VW:VW + T * H].rearrange("p (t h) -> p t h", t=T), gr[:, :, :], 0.0, None,
                                        ALU.max).then_inc(s["vdone"], 1)
                if at.plus(2).exists():
                    normalise(at.plus(2))

            run(dve, step, 2, B)


def stage_attend(nc, m, k, d):
    K, Q, VG = k["k"], k["q"], k["vg"]
    QD = k["qd"]
    PR = [m.sb(f"b_p{p}", [P, T, H, P]) for p in range(2)]
    WM = m.sb("b_wm", [P, 2, P // (2 * WR * WB), H, WB])
    VR = [m.sb(f"b_vr{p}", [P, S]) for p in range(2)]
    XT = m.sb("b_xt", [P, NQ4 * P])
    XN = [m.sb(f"b_xn{p}", [P, E]) for p in range(2)]
    RD = m.sb("b_rd", [P, H])
    MX = [m.sb(f"b_mx{p}", [P, H]) for p in range(2)]
    nm, r1, r2 = (m.sb(f"b_{n}", [P, H]) for n in ("nm", "r1", "r2"))
    NP = m.sb("b_np", [P, 6, H], BF16)
    MT = m.sb("b_mt", [6 * H, P], BF16)
    idb = m.sb("b_idb", [P, P], BF16)
    SC = [m.ps(f"b_s{p}", [P, 2, S]) for p in range(2)]
    PA = [m.ps(f"b_a{p}", [P, S]) for p in range(2)]
    PV = m.ps("b_pv", [P, NQ4 * P])
    MI = m.ps("b_mi", [P, S])
    names = ("init", "a_ready", "a_used", "s_ready", "p_ready", "w_ready", "w_masked", "pv_ready", "xt_ready", "rd",
             "mp_ready", "mt_ready", "mt_copied", "xtt_ready", "norm", "m_out", "m_in", "xo_out0", "xo_out1",
             "qd_ready", "v_ready", "dv", "v_in0", "v_in1")
    s = {n: m.sem("b_s_" + n) for n in names}
    v_in, xo_out = ([s[f"{n}{p}"] for p in range(2)] for n in ("v_in", "xo_out"))
    kq_in = k["kq_in"]
    NKQ = PARTS + SLOTS
    MCH = 6
    SCALE = float(1.0 / np.sqrt(np.float32(HD)))

    PER = 2 * T

    def at0(c):
        return At(0, c, PER, U)

    def window(t, i):
        return abs(t - i) <= 1

    def blocks(t, i, g):
        half = P // QB // 2
        near = {0: range(half * g, half * (g + 1)), -1: range(REL // QB), 1: range((P - REL) // QB, P // QB)}
        return near.get(t - i, range(0))

    def row_heads(i, c):
        other = (32, 48, 56, 40, 56, 24, 24, 40)
        scores = [(2 if n // NG == i else 1) * H + len(blocks(n // NG, i, n % NG)) for n in range(SUB)]
        work = np.cumsum([0] + [a + b for a, b in zip(scores, other)])
        first, last = (int(round(H * w / work[-1])) for w in work[c:c + 2])
        return range(first, last)

    with nc.Block() as block:
        @block.sync
        def _(sp):
            def load_v(at):
                p = (at.c // T) % 2
                batch = bass.ds(at.it * 2 + at.c // T, 1)
                sp.dma_start(VR[p][:, :], d["v"][batch].rearrange("o p c -> (o p) c")).then_inc(v_in[p], 16)
                sp.dma_start(VG[p][:, VW:], d["guard"][batch].rearrange("o p c -> (o p) c")).then_inc(v_in[p], 16)

            def guard_rows(at):
                sp.wait_ge(s["mt_copied"], at.count(1, 1))
                sp.dma_start(d["gt"][at.c % 2], MT[:, :]).then_inc(s["m_out"], 16)
                sp.wait_ge(s["m_out"], at.count(16, 16))
                p, i = (at.c // T) % 2, at.c % T
                sp.dma_start(Q[p][GROW:ROWS, :, i * P:(i + 1) * P], d["gt"][at.c % 2].rearrange("(c h) q -> c h q", h=H))\
                    .then_inc(s["m_in"], 16)

            load_v(at0(0))
            load_score_operands(sp, k, d, 1, 1)
            load_v(at0(T))
            guard_rows(at0(0))

            def unit(at):
                if at.c % T == 0 and at.since(T) and at.plus(T).exists():
                    sp.wait_ge(s["s_ready"], at.count(SUB))
                    load_score_operands(sp, k, d, at.it * 2 + at.c // T + 1, (at.c // T + 1) % 2)
                    sp.wait_ge(s["w_ready"], at.count(2))
                    load_v(at.plus(T))
                if at.since(2):
                    sp.wait_ge(s["norm"], at.count(1, -1))
                    sp.dma_start(d["xo"][bass.ds(at.count(1, -2), 1)].rearrange("o p c -> (o p) c"), XN[at.c % 2][:, :])\
                        .then_inc(xo_out[at.c % 2], 16)
                if at.plus(1).exists():
                    guard_rows(at.plus(1))

            run(sp, unit, PER, U)
            for u in (U - 2, U - 1):
                sp.wait_ge(s["norm"], u + 1)
                sp.dma_start(d["xo"][u], XN[u % 2][:, :]).then_inc(xo_out[u % 2], 16)
            for p in range(2):
                sp.wait_ge(xo_out[p], 16 * U // 2)

        @block.gpsimd
        def _(pool):
            def unit(at):
                p, i = (at.c // T) % 2, at.c % T
                one = bc(k["one"][0:OPR, 0:1].to_broadcast([OPR, H]), 2, P // QB)
                if i == 0:
                    pool.wait_ge(kq_in[p], (at.even(T) + 1) * (16 * NKQ))
                if at.since(2):
                    pool.wait_ge(s["s_ready"], at.count(SUB, -SUB))
                if i == 1:
                    pool.wait_ge(s["v_ready"], at.it * 2 + (at.c // T + 1))
                for j in range(QB):
                    src = Q[p][0:OPR, :, i * P + j:(i + 1) * P:QB]
                    ins = nc.gpsimd.tensor_tensor(QD[at.c % 2][QROW * j:QROW * j + OPR, :, j:P:QB], src, one, ALU.mult)
                ins.then_inc(s["qd_ready"], 1)
                if i == 0:
                    pool.wait_ge(s["qd_ready"], at.count(1, 1))
                    pool.wait_ge(v_in[p], (at.even(T) + 1) * 32)
                    for side in range(2):
                        v = VG[p][:, side * VW // 2:(side + 1) * VW // 2].rearrange("p (t h c) -> p t h c", t=T, h=H)
                        ins = nc.gpsimd.tensor_tensor(v[:, :, :, 0:HD], VR[p][:, :].rearrange("p (t h d) -> p t h d", t=T, h=H),
                                                      bc(k["bv2"][:, side, :].rearrange("p (h d) -> p h d", h=H), 1, T), ALU.add)
                    ins.then_inc(s["v_ready"], 1)

            run(pool, unit, PER, U)

        @block.tensor
        def _(pe):
            def row_scores(at, heads):
                p, i = (at.c // T) % 2, at.c % T
                if at.c % T == 0 and heads[0] == 0:
                    pe.wait_ge(kq_in[p], (at.even(T) + 1) * (16 * NKQ))
                for h in heads:
                    if at.since(1) or h >= 2:
                        pe.wait_ge(s["a_used"], at.count(H, h - 1))
                    nc.tensor.matmul(PA[h % 2][:, :], Q[p][0:GROW, h, i * P:(i + 1) * P], K[p][0:GROW, h, :],
                                     start=True, stop=True).then_inc(s["a_ready"], 1)

            def scores(at, c):
                t, g, i, p = c // NG, c % NG, at.c % T, (at.c // T) % 2
                out = SC[c % 2]
                if at.since(1) or c >= 2:
                    pe.wait_ge(s["p_ready"], at.count(SUB, c - 1))
                if c == 0:
                    pe.wait_ge(s["m_in"], at.count(16, 16))
                rows = DROW if t <= i else ROWS
                for h in range(H) if t == i else range(HG * g, HG * g + HG):
                    lhs, hh = K[p][0:rows, h, t * P:(t + 1) * P], h % HG
                    if t == i:
                        pieces = [(n, h * 32, 32, 64 * g + 32 * n) for n in range(2)]
                    elif window(t, i):
                        pieces = [(n, hh * 64, 64, 64 * n) for n in range(2)]
                    else:
                        pieces = [(hh // 4, hh % 4 * P, P, 0)]
                    for n, col, width, q0 in pieces:
                        ins = nc.tensor.matmul(out[:, n, col:col + width], lhs, Q[p][0:rows, h, i * P + q0:i * P + q0 + width],
                                               start=col == 0, stop=True, skip_group_check=True)
                if window(t, i):
                    if c == NG * max(i - 1, 0):
                        pe.wait_ge(s["qd_ready"], at.count(1, 1))
                    heads, nq = (range(H), 32) if t == i else (range(HG * g, HG * g + HG), 64)
                    for b in blocks(t, i, g):
                        x0 = (ZLO_0 if t <= i else ZLO_W + ZHI_0) + (t - i) * P - QB * b
                        o = out[:, QB * b // nq % 2, :].rearrange("p (h q) -> p h q", q=nq)[:, :, QB * b % nq:QB * b % nq + QB]
                        ins = nc.tensor.matmul(o, k["z"][0:QROWS, x0:x0 + P],
                                               QD[at.c % 2][0:QROWS, heads[0]:heads[-1] + 1, b * QB:(b + 1) * QB],
                                               start=False, stop=True, skip_group_check=True)
                ins.then_inc(s["s_ready"], 1)

            def value_products(at, t):
                i, p = at.c % T, (at.c // T) % 2
                v = VG[p][:, 0:VW].rearrange("p (s t h c) -> p s t h c", s=2, t=T, h=H)
                if t == 0 and at.since(1):
                    pe.wait_ge(s["xt_ready"], at.count(1))
                if t == 0 and i == 0:
                    pe.wait_ge(s["v_ready"], at.it * 2 + (at.c // T + 1))
                pe.wait_ge(s["p_ready"], at.count(SUB, NG * (t + 1)))
                for g in range(H // NQ4):
                    for a in range(NQ4):
                        h = NQ4 * a + g
                        nc.tensor.matmul(PV[32 * a:32 * a + V16, g * P:(g + 1) * P], v[:, 0 if t <= i else 1, t, h, :],
                                         PR[at.c % 2][:, t, h, :], start=(t == 0 and g == 0), stop=True,
                                         skip_group_check=True)

            def relative_values(at, half):
                i = at.c % T
                for n in range(P // (2 * WB)):
                    qb = half * P // (2 * WB) + n
                    jobs = [(i, k["tvd"], P - WB - WB * qb)]
                    if i > 0 and qb < CW // WB:
                        jobs.append((i - 1, k["tvm"], CW - WB - WB * qb))
                    if i < T - 1 and qb >= (P - CW) // WB:
                        jobs.append((i + 1, k["tvp"], P - WB - WB * qb))
                    r0, grp = (n % WR) * WB * HD, n // WR
                    for j, (t, tab, q0) in enumerate(jobs):
                        ins = nc.tensor.matmul(MI[r0:r0 + WB * HD, grp * H * WB:(grp + 1) * H * WB],
                                               tab[:, q0 * HD:(q0 + WB) * HD], PR[at.c % 2][:, t, :, qb * WB:(qb + 1) * WB],
                                               start=j == 0, stop=j == len(jobs) - 1)
                ins.then_inc(s["w_ready"], 1)

            def relative_value_sums(at):
                pe.wait_ge(s["w_masked"], at.count(2, 2))
                for b in range(WR):
                    for a in range(NQ4):
                        o = PV[32 * a:32 * a + V16, :].rearrange("p (h g b q) -> p h g b q", h=NQ4, b=WR, q=WB)[:, :, :, b, :]
                        w = WM[:, :, :, NQ4 * a:NQ4 * a + NQ4, :].rearrange("p c g h q -> p h (c g) q")
                        ins = nc.tensor.matmul(o, k["red"][:, b, :], w, start=False, stop=True, skip_group_check=True)
                ins.then_inc(s["pv_ready"], 1)

            def guard_transpose(at):
                pe.wait_ge(s["mp_ready"], at.count(1, 1))
                nc.tensor.transpose(MIB, NP[:, :, :].rearrange("p c h -> p (c h)"), idb[:, :]).then_inc(s["mt_ready"], 1)

            def output_transposes(at):
                pe.wait_ge(s["xt_ready"], at.count(1, 1))
                for g in range(NQ4):
                    ins = nc.tensor.transpose(MI[:, g * P:(g + 1) * P], XT[:, g * P:(g + 1) * P], k["ident"][:, :])
                ins.then_inc(s["xtt_ready"], 1)

            MIB = MI[0:6 * H, 0:P // 2].bitcast(BF16)
            pe.wait_ge(s["init"], 1)
            row_scores(at0(0), range(H))
            guard_transpose(at0(0))
            row_scores(at0(1), range(H))

            def unit(at):
                before = at.plus(-1)
                for c in range(SUB):
                    heads = row_heads(at.c % T, c) if at.plus(2).exists() else ()
                    if heads:
                        row_scores(at.plus(2), heads[:1])
                    scores(at, c)
                    if heads[1:]:
                        row_scores(at.plus(2), heads[1:2])
                    if before.exists():
                        if c == 0:
                            value_products(before, T - 1)
                        if c == 1:
                            if at.since(2):
                                pe.wait_ge(s["norm"], at.count(1, -1))
                            else:
                                pe.wait_ge(s["mt_copied"], 2)
                            relative_values(before, 0)
                        if c == 2:
                            pe.wait_ge(s["w_masked"], before.count(2, 1))
                            relative_values(before, 1)
                        if c == 3:
                            relative_value_sums(before)
                    if c == 3 and at.plus(1).exists():
                        if not at.since(1):
                            pe.wait_ge(s["mt_copied"], 1)
                        guard_transpose(at.plus(1))
                    if c == 4:
                        if before.exists():
                            if at.plus(1).exists():
                                pe.wait_ge(s["mt_copied"], at.count(1, 2))
                            output_transposes(before)
                        value_products(at, 0)
                    if c == 5:
                        value_products(at, 1)
                    if c == 7:
                        value_products(at, 2)
                    if heads[2:]:
                        row_scores(at.plus(2), heads[2:])

            run(pe, unit, PER, U)
            end = at0(U - 1)
            value_products(end, T - 1)
            pe.wait_ge(s["norm"], U - 1)
            relative_values(end, 0)
            pe.wait_ge(s["w_masked"], 2 * U - 1)
            relative_values(end, 1)
            relative_value_sums(end)
            output_transposes(end)

        @block.scalar
        def _(act):
            def exponentials(at, c):
                t, g, i = c // NG, c % NG, at.c % T
                act.wait_ge(s["s_ready"], at.count(SUB, c + 1))
                if c == 0 and at.since(2):
                    act.wait_ge(s["w_ready"], at.count(2, -2))
                out = PR[at.c % 2][:, t, HG * g:HG * g + HG, :]
                if t == i:
                    src = SC[c % 2][:, :, :].rearrange("p c (h q) -> p c h q", h=H)
                    out = PR[at.c % 2][:, t, :, 64 * g:64 * g + 64].rearrange("p h (c q) -> p c h q", c=2)
                elif window(t, i):
                    src = SC[c % 2][:, :, :].rearrange("p c (h q) -> p c h q", h=HG)
                    out = out.rearrange("p h (c q) -> p c h q", c=2)
                else:
                    src = SC[c % 2][:, :, :].rearrange("p c (h q) -> p (c h) q", q=P)
                nc.scalar.activation(out, src, ACT.Exp, scale=SCALE).then_inc(s["p_ready"], 1)

            def guard_copy(at):
                act.wait_ge(s["mt_ready"], at.count(1, 1))
                if at.since(1):
                    act.wait_ge(s["m_out"], at.count(16))
                nc.scalar.copy(MT[:, :], MI[0:6 * H, 0:P // 2].bitcast(BF16)).then_inc(s["mt_copied"], 1)

            def output_copy(at):
                act.wait_ge(s["pv_ready"], at.count(1, 1))
                if at.since(1):
                    act.wait_ge(s["xtt_ready"], at.count(1))
                nc.scalar.copy(XT[:, :], PV[:, :]).then_inc(s["xt_ready"], 1)

            guard_copy(at0(0))

            def unit(at):
                for c in range(SUB):
                    exponentials(at, c)
                    if c == 3 and at.plus(-1).exists():
                        output_copy(at.plus(-1))
                    if c == 3 and at.plus(1).exists():
                        guard_copy(at.plus(1))

            run(act, unit, PER, U)
            output_copy(at0(U - 1))

        @block.vector
        def _(dve):
            nc.vector.memset(PV[:, :], 0.0)
            nc.vector.tensor_copy(idb[:, :], k["ident"][:, :]).then_inc(s["init"], 1)

            def row_max(at, heads):
                for h in heads:
                    dve.wait_ge(s["a_ready"], at.count(H, h + 1))
                    nc.vector.reduce_max(MX[at.c % 2][:, h:h + 1], PA[h % 2][:, :], AX_X).then_inc(s["a_used"], 1)

            def link(at, n, ins):
                ins.then_inc(s["dv"], 1)
                dve.wait_ge(s["dv"], at.count(MCH - 1, n))

            def guard_parts(at):
                p, i = (at.c // T) % 2, at.c % T
                dve.wait_ge(s["a_used"], at.count(H, H))
                if i == 0:
                    dve.wait_ge(v_in[p], (at.even(T) + 1) * 32)
                if at.since(1):
                    dve.wait_ge(s["mt_ready"], at.count(1))
                g = VG[p][:, VW + i * H:VW + (i + 1) * H]
                nc.vector.tensor_copy(NP[:, 3:6, :], VG[p][:, VW + T * H:VGW].rearrange("p (c t h) -> p c t h", c=3, t=T)[:, :, i, :])
                link(at, 1, nc.vector.scalar_tensor_tensor(out=nm[:, :], in0=MX[at.c % 2][:, :], scalar=-1.0, in1=g,
                                                           op0=ALU.mult, op1=ALU.subtract))
                link(at, 2, nc.vector.tensor_copy(NP[:, 0, :], nm[:, :]))
                link(at, 3, nc.vector.tensor_tensor(r1[:, :], nm[:, :], NP[:, 0, :], ALU.subtract))
                link(at, 4, nc.vector.tensor_copy(NP[:, 1, :], r1[:, :]))
                link(at, 5, nc.vector.tensor_tensor(r2[:, :], r1[:, :], NP[:, 1, :], ALU.subtract))
                nc.vector.tensor_copy(NP[:, 2, :], r2[:, :]).then_inc(s["mp_ready"], 1)

            def keep_values(at, half):
                dve.wait_ge(s["w_ready"], at.count(2, half + 1))
                if at.since(1):
                    dve.wait_ge(s["pv_ready"], at.count(1))
                nc.vector.tensor_tensor(WM[:, half, :, :, :].rearrange("p g h q -> p (g h) q"),
                                        MI[:, :].rearrange("p (n q) -> p n q", q=WB),
                                        bc(k["wmask"][:, :], 1, S // WB), ALU.mult).then_inc(s["w_masked"], 1)

            def normalise(at):
                dve.wait_ge(s["xtt_ready"], at.count(1, 1))
                v = MI[:, :].rearrange("p (n c) -> p n c", c=32)
                nc.vector.reciprocal(RD[:, :], v[:, :, HD]).then_inc(s["rd"], 1)
                dve.wait_ge(s["rd"], at.count(1, 1))
                if at.since(2):
                    dve.wait_ge(xo_out[at.c % 2], at.even(1) * 16)
                xn = XN[at.c % 2][:, :].rearrange("p (a g d) -> p g a d", a=NQ4, d=HD)
                nc.vector.tensor_tensor(xn, MI[:, :].rearrange("p (g a c) -> p g a c", g=NQ4, a=NQ4)[:, :, :, 0:HD],
                                        bc(RD[:, :].rearrange("p (g a) -> p g a", g=NQ4), 3, HD), ALU.mult).then_inc(s["norm"], 1)

            row_max(at0(0), range(H))
            guard_parts(at0(0))
            row_max(at0(1), range(H))

            def unit(at):
                before = at.plus(-1)
                if at.plus(1).exists():
                    guard_parts(at.plus(1))
                for c in range(SUB):
                    heads = row_heads(at.c % T, c) if at.plus(2).exists() else ()
                    row_max(at.plus(2), heads[:2])
                    if before.exists():
                        if c in (1, 2):
                            keep_values(before, c - 1)
                        if c == 4:
                            normalise(before)
                    row_max(at.plus(2), heads[2:])

            run(dve, unit, PER, U)
            end = at0(U - 1)
            keep_values(end, 0)
            keep_values(end, 1)
            normalise(end)


def stage_output(nc, m, k, d):
    XA, X, X1 = ([m.sb(f"c_{n}{p}", [P, T, E]) for p in range(2)] for n in ("xa", "x", "x1"))
    XNT = [m.sb(f"c_xnT{p}", [P, S]) for p in range(2)]
    xn, fin, aT = m.sb("c_xn", [P, T, E]), m.sb("c_fin", [P, T, E]), m.sb("c_aT", [P, S])
    sg, hh = m.sb("c_sg", [P, FC, S]), m.sb("c_hh", [P, FC, S])
    tmp = {"st": m.sb("c_st", [P, T, 6]), "mv": m.sb("c_mv", [P, T, 2]), "std": m.sb("c_std", [P, T]),
           "rstd": m.sb("c_rstd", [P, T]), "gap": m.sb("c_gap", [P, 1])}
    pA, pT, py, po = (m.ps(f"c_p{n}", [P, S]) for n in ("a", "t", "y", "o"))
    PG, PU = ([m.ps(f"c_p{n}{p}", [P, S]) for p in range(2)] for n in "gu")
    names = ("in0", "in1", "xb", "aT", "aTs", "y", "x1", "var", "eps", "rstd", "xn", "xT", "xTs", "gate", "up", "silu", "hid",
             "down", "fin", "out", "dv")
    s = {n: m.sem("c_s_" + n) for n in names}
    x_in = [s[f"in{p}"] for p in range(2)]

    def at0(c):
        return At(0, c, 2, B)

    with nc.Block() as block:
        @block.sync
        def _(sp):
            def load(at):
                p = at.c % 2
                sp.dma_start(XA[p][:, :, :], d["xo"][bass.ds(at.count(T), T)].rearrange("t p e -> p t e")).then_inc(x_in[p], 16)
                sp.dma_start(X[p][:, :, :], d["x"][bass.ds(at.count(), 1)].rearrange("o (t p) e -> p (o t) e", p=P)).then_inc(x_in[p], 16)

            load(at0(0))
            load(at0(1))

            def step(at):
                if at.plus(2).exists():
                    sp.wait_ge(s["x1"], at.count(1, 1))
                    load(at.plus(2))
                sp.wait_ge(s["fin"], at.count(1, 1))
                sp.dma_start(d["out"][bass.ds(at.count(), 1)].rearrange("o (t p) e -> p (o t) e", p=P), fin[:, :, :]).then_inc(s["out"], 16)

            run(sp, step, 2, B)
            sp.wait_ge(s["out"], 16 * B)

        @block.gpsimd
        def _(pool):
            def biased(at):
                x = X[at.c % 2]
                pool.wait_ge(x_in[at.c % 2], at.even(1) * 32 + 32)
                nc.gpsimd.tensor_tensor(x[:, :, :], x[:, :, :], bc(k["bo"][:, :], 1, T), ALU.add).then_inc(s["xb"], 1)

            def deviation(at):
                inverse_deviation(nc, pool, k, tmp, at, s["var"], s["eps"], s["rstd"])

            biased(at0(0))
            deviation(at0(0))
            biased(at0(1))

            def step(at):
                if at.plus(1).exists():
                    deviation(at.plus(1))
                if at.plus(2).exists():
                    biased(at.plus(2))

            run(pool, step, 2, B)

        @block.tensor
        def _(pe):
            def attention_transposes(at):
                pe.wait_ge(x_in[at.c % 2], at.even(1) * 32 + 32)
                if at.since(1):
                    pe.wait_ge(s["aTs"], at.count())
                for t in range(T):
                    ins = nc.tensor.transpose(pA[:, t * P:(t + 1) * P], XA[at.c % 2][:, t, :], k["ident"][:, :])
                ins.then_inc(s["aT"], 1)

            def output_projection(at):
                pe.wait_ge(s["aTs"], at.count(1, 1))
                if at.since(1):
                    pe.wait_ge(s["x1"], at.count())
                for t in range(T):
                    ins = nc.tensor.matmul(py[:, t * P:(t + 1) * P], aT[:, t * P:(t + 1) * P], k["wo"][:, :], start=True, stop=True)
                ins.then_inc(s["y"], 1)

            def row_transposes(at):
                pe.wait_ge(s["xn"], at.count(1, 1))
                if at.since(1):
                    pe.wait_ge(s["xTs"], at.count())
                for t in range(T):
                    ins = nc.tensor.transpose(pT[:, t * P:(t + 1) * P], xn[:, t, :], k["ident"][:, :])
                ins.then_inc(s["xT"], 1)

            def gate_and_up(at, c):
                n = (at.c * FC + c) % 2
                if c == 0:
                    pe.wait_ge(s["xTs"], at.count(1, 1))
                if c >= 2 or at.since(1):
                    pe.wait_ge(s["hid"], at.count(FC, c - 1))
                nc.tensor.matmul(PG[n][:, :], k["wg"][:, c * P:(c + 1) * P], XNT[at.c % 2][:, :], start=True, stop=True).then_inc(s["gate"], 1)
                nc.tensor.matmul(PU[n][:, :], k["wu"][:, c * P:(c + 1) * P], XNT[at.c % 2][:, :], start=True, stop=True).then_inc(s["up"], 1)

            def down(at, c):
                pe.wait_ge(s["hid"], at.count(FC, c + 1))
                if c == 0 and at.since(1):
                    pe.wait_ge(s["fin"], at.count())
                for t in range(T):
                    ins = nc.tensor.matmul(po[:, t * P:(t + 1) * P], hh[:, c, t * P:(t + 1) * P], k["wd"][:, c, :],
                                           start=c == 0 and t == 0, stop=c == FC - 1, skip_group_check=True)
                if c == FC - 1:
                    ins.then_inc(s["down"], 1)

            attention_transposes(at0(0))
            output_projection(at0(0))
            attention_transposes(at0(1))
            row_transposes(at0(0))

            def step(at):
                after = at.plus(1)
                gate_and_up(at, 0)
                if after.exists():
                    output_projection(after)
                for c in range(1, FC):
                    gate_and_up(at, c)
                for c in range(FC):
                    down(at, c)
                if after.exists():
                    row_transposes(after)
                if at.plus(2).exists():
                    attention_transposes(at.plus(2))

            run(pe, step, 2, B)

        @block.scalar
        def _(act):
            def transposed_attention(at):
                act.wait_ge(s["aT"], at.count(1, 1))
                if at.since(1):
                    act.wait_ge(s["y"], at.count())
                nc.scalar.copy(aT[:, :], pA[:, :]).then_inc(s["aTs"], 1)

            def transposed_rows(at):
                act.wait_ge(s["xT"], at.count(1, 1))
                nc.scalar.copy(XNT[at.c % 2][:, :], pT[:, :]).then_inc(s["xTs"], 1)

            transposed_attention(at0(0))
            transposed_attention(at0(1))
            transposed_rows(at0(0))

            def step(at):
                for c in range(FC):
                    act.wait_ge(s["gate"], at.count(FC, c + 1))
                    if at.since(1):
                        act.wait_ge(s["hid"], at.count(FC, c - FC + 1))
                    nc.scalar.activation(sg[:, c, :], PG[(at.c * FC + c) % 2][:, :], ACT.Silu).then_inc(s["silu"], 1)
                if at.plus(1).exists():
                    transposed_rows(at.plus(1))
                if at.plus(2).exists():
                    transposed_attention(at.plus(2))

            run(act, step, 2, B)

        @block.vector
        def _(dve):
            def residual(at):
                p = at.c % 2
                if at.since(2):
                    dve.wait_ge(s["fin"], at.count(1, -1))
                dve.wait_ge(s["y"], at.count(1, 1))
                dve.wait_ge(s["xb"], at.count(1, 1))
                nc.vector.tensor_tensor(X1[p][:, :, :], py[:, :].rearrange("p (t e) -> p t e", t=T), X[p][:, :, :], ALU.add).then_inc(s["x1"], 1)
                dve.wait_ge(s["x1"], at.count(1, 1))

                def link(ins):
                    ins.then_inc(s["dv"], 1)
                    dve.wait_ge(s["dv"], at.count(1, 1))

                layernorm_statistics(nc, X1[p], tmp, link, s["var"])

            def normalise(at):
                dve.wait_ge(s["rstd"], at.count(1, 1))
                if at.since(1):
                    dve.wait_ge(s["xT"], at.count())
                layernorm_rows(nc, X1[at.c % 2], xn, tmp).then_inc(s["xn"], 1)

            def hidden(at, c):
                dve.wait_ge(s["silu"], at.count(FC, c + 1))
                dve.wait_ge(s["up"], at.count(FC, c + 1))
                if at.since(1):
                    dve.wait_ge(s["down"], at.count())
                nc.vector.tensor_tensor(hh[:, c, :], sg[:, c, :], PU[(at.c * FC + c) % 2][:, :], ALU.mult).then_inc(s["hid"], 1)

            residual(at0(0))
            normalise(at0(0))

            def step(at):
                after = at.plus(1)
                hidden(at, 0)
                if after.exists():
                    residual(after)
                hidden(at, 1)
                if after.exists():
                    normalise(after)
                hidden(at, 2)
                dve.wait_ge(s["down"], at.count(1, 1))
                if at.since(1):
                    dve.wait_ge(s["out"], at.count(16))
                nc.vector.tensor_tensor(fin[:, :, :], po[:, :].rearrange("p (t e) -> p t e", t=T), X1[at.c % 2][:, :, :],
                                        ALU.add).then_inc(s["fin"], 1)

            run(dve, step, 2, B)


def program(nc, d):
    for name, shape, dt in (("qop", (B, PARTS, P, S), BF16), ("kop", (B, PARTS, P, S), BF16),
                            ("v", (B, P, S), F32), ("guard", (B, P, VGW - VW), F32), ("xo", (U, P, E), F32),
                            ("gt", (2, 6 * H, P), BF16)):
        d[name] = nc.dram_tensor("scratch_" + name, shape, dt, kind="Internal").ap()
    with ExitStack() as keep:
        m = Memory(nc, keep)
        k = {"ident": m.sb("ident", [P, P]), "wmask": m.sb("wmask", [P, WB]),
             "red": m.sb("red", [P, WR, V16]), "z": m.sb("z", [P, ZLO_W + ZHI_W], BF16),
             "tvd": m.sb("tvd", [P, P * HD]), "tvm": m.sb("tvm", [P, CW * HD]), "tvp": m.sb("tvp", [P, CW * HD]),
             "wq": m.sb("wq", [P, P]), "wk": m.sb("wk", [P, P]), "wv": m.sb("wv", [P, P]), "wo": m.sb("wo", [P, P]),
             "bq": m.sb("bq", [P, 1]), "bk0": m.sb("bk0", [P, 1]), "relend": m.sb("relend", [P, H]),
             "bv2": m.sb("bv2", [P, 2, P]), "bo": m.sb("bo", [P, P]), "relbd": m.sb("relbd", [P, 2, H * REL], BF16),
             "wg": m.sb("wg", [P, F]), "wu": m.sb("wu", [P, F]), "wd": m.sb("wd", [P, FC, P]),
             "eps": m.sb("eps", [P, 1]), "root": m.sb("root", [P, 1]), "one": m.sb("one", [P, 1]),
             "minus": m.sb("minus", [P, P], BF16),
             "kq_in": [m.sem(f"kq_in{p}") for p in range(2)],
             "k": [m.sb(f"k{p}", [P, H, S], BF16) for p in range(2)],
             "q": [m.sb(f"q{p}", [P, H, S], BF16) for p in range(2)],
             "qd": [m.sb(f"qd{p}", [P, H, P], BF16) for p in range(2)],
             "vg": [m.sb(f"vg{p}", [P, VGW]) for p in range(2)]}
        for stage in (setup_constants, stage_project, stage_attend, stage_output):
            with ExitStack() as ctx:
                stage(nc, Memory(nc, ctx), k, d)


def kernel(**inputs):
    import concourse.bacc as _bacc
    from concourse.bass_utils import run_bass_kernel_spmd as _run

    a = {n.removeprefix("L0_"): np.asarray(v) for n, v in inputs.items()}
    rel_k, rel_v = a["attn_rel_k"], a["attn_rel_v"]

    def by_d(w):
        return w.reshape(H, HD, *w.shape[1:]).swapaxes(0, 1).reshape(P, *w.shape[1:])

    clipped = np.clip(np.arange(-EXT_0, EXT_0 + 1), -REL, REL) + REL
    arrays = {
        "x": a["attn_hidden_states"],
        "wq": by_d(a["attn_Wq"]).T, "wk": by_d(a["attn_Wk"]).T, "wv": a["attn_Wv"].T, "wo": a["attn_Wo"].T,
        "bq": by_d(a["attn_bq"])[:, None], "bk": by_d(a["attn_bk"])[:, None],
        "bv": a["attn_bv"][None, :], "bo": a["attn_bo"][None, :],
        "rkh": np.repeat(rel_k.T, H, axis=0),
        "rkj": np.tile(rel_k[[0, NREL - 1]].T, (SLOTS, 1)),
        "slot": np.repeat([[n in K_SLOT[part] for part in range(PARTS)] for n in range(SLOTS)], HD, axis=0).astype(np.float32),
        "rkx": rel_k[clipped].T, "rvx": rel_v[clipped], "rv": rel_v,
        "wg": a["ffn_w_gate"].T, "wu": a["ffn_w_up"].T, "wd": a["ffn_w_down"].T,
    }
    arrays = {"in_" + n: np.ascontiguousarray(v) for n, v in arrays.items()}
    nc = _bacc.Bacc("TRN2", target_bir_lowering=False, num_devices=1)
    d = {n[3:]: nc.dram_tensor(n, v.shape, mybir.dt.from_np(v.dtype), kind="ExternalInput").ap() for n, v in arrays.items()}
    d["out"] = nc.dram_tensor("out", (B, S, E), F32, kind="ExternalOutput").ap()
    program(nc, d)
    r = _run(nc, [arrays], core_ids=[0])
    return r.results[0]["out"]
```
